# Optimizing a Trainium2 kernel written in Bass

```python
import numpy as np
import jax
import jax.numpy as jnp

def _softmax(x, axis=-1):
    return jax.nn.softmax(x, axis=axis)

def _gelu(x):
    return jax.nn.gelu(x, approximate=True)

def _silu(x):
    return jax.nn.silu(x)

def _sigmoid(x):
    return jax.nn.sigmoid(x)

def _layernorm(x, axis=-1, eps=1e-05):
    m = jnp.mean(x, axis=axis, keepdims=True)
    v = jnp.var(x, axis=axis, keepdims=True)
    return (x - m) / jnp.sqrt(v + eps)

def _scatter_add(tgt, idx, src, axis=0):
    return tgt.at[idx].add(src)

def _segment_sum(src, seg, n):
    return jax.ops.segment_sum(src, seg, n)
kernel_name = 'mk_sandwich_d1_jaxref_r8_3e604d'

def setup_inputs(seed: int=0):
    np.random.seed(seed)
    _w = jnp.asarray

    def _L0_attn_setup():
        import jax, jax.numpy as jnp
        import numpy as np
        DIM = 128
        B, T = (8, 128)

        def _wkv(w, u, k, v):
            e_dec = jnp.exp(-w)
            e_grow = jnp.exp(w)
            Tlen = k.shape[1]
            cnt = jnp.maximum(jnp.arange(Tlen) - 1, 0).astype(k.dtype)
            msk = (jnp.arange(Tlen) > 0).astype(k.dtype)

            def step(carry, inp):
                A, Bacc = carry
                kt, vt, ct, mt = inp
                out = A + jnp.exp(u + kt) * (vt * Bacc + ct)
                ek = jnp.exp(kt)
                A = e_dec * A + mt * ek * vt
                Bacc = e_grow * Bacc + mt / ek
                return ((A, Bacc), out)
            kT = jnp.moveaxis(k, 1, 0)
            vT = jnp.moveaxis(v, 1, 0)
            z = jnp.zeros_like(k[:, 0])
            _, outs = jax.lax.scan(step, (z, z), (kT, vT, cnt, msk))
            return jnp.moveaxis(outs, 0, 1)
        key = jax.random.key(seed)
        ks = jax.random.split(key, 10)
        s = 0.02
        x = jax.random.normal(ks[0], (B, T, DIM), dtype=jnp.float32)
        Wr = jax.random.normal(ks[1], (DIM, DIM), dtype=jnp.float32) * s
        Wk = jax.random.normal(ks[2], (DIM, DIM), dtype=jnp.float32) * s
        Wv = jax.random.normal(ks[3], (DIM, DIM), dtype=jnp.float32) * s
        Wo = jax.random.normal(ks[4], (DIM, DIM), dtype=jnp.float32) * s
        r_mu = jax.random.uniform(ks[5], (DIM,), dtype=jnp.float32)
        k_mu = jax.random.uniform(ks[6], (DIM,), dtype=jnp.float32)
        v_mu = jax.random.uniform(ks[7], (DIM,), dtype=jnp.float32)
        w = jax.random.uniform(ks[8], (DIM,), dtype=jnp.float32) * 0.005
        u = jax.random.normal(ks[9], (DIM,), dtype=jnp.float32) * 0.1
        return {'x': x, 'Wr': Wr, 'Wk': Wk, 'Wv': Wv, 'Wo': Wo, 'r_mu': r_mu, 'k_mu': k_mu, 'v_mu': v_mu, 'w': w, 'u': u}
    _L0_attn_in = _L0_attn_setup()

    def _L0_ffn_setup():
        import jax, jax.numpy as jnp
        import numpy as np
        B, S, D, F, E, NS, K = (2, 128, 128, 512, 8, 8, 2)
        FS = F // NS
        key = jax.random.key(seed)
        ks = jax.random.split(key, 8)
        scale = 0.02
        return {'hidden_states': jax.random.normal(ks[0], (B, S, D), jnp.float32), 'gate_W': jax.random.normal(ks[1], (E, D), jnp.float32) * scale, 'w1_e': jax.random.normal(ks[2], (E, D, F), jnp.float32) * scale, 'w3_e': jax.random.normal(ks[3], (E, D, F), jnp.float32) * scale, 'w2_e': jax.random.normal(ks[4], (E, F, D), jnp.float32) * scale, 'w1_s': jax.random.normal(ks[5], (NS, D, FS), jnp.float32) * scale, 'w3_s': jax.random.normal(ks[6], (NS, D, FS), jnp.float32) * scale, 'w2_s': jax.random.normal(ks[7], (NS, FS, D), jnp.float32) * scale}
    _L0_ffn_in = _L0_ffn_setup()
    _d = {'L0_attn_x': _L0_attn_in['x'], 'L0_attn_Wr': _L0_attn_in['Wr'], 'L0_attn_Wk': _L0_attn_in['Wk'], 'L0_attn_Wv': _L0_attn_in['Wv'], 'L0_attn_Wo': _L0_attn_in['Wo'], 'L0_attn_r_mu': _L0_attn_in['r_mu'], 'L0_attn_k_mu': _L0_attn_in['k_mu'], 'L0_attn_v_mu': _L0_attn_in['v_mu'], 'L0_attn_w': _L0_attn_in['w'], 'L0_attn_u': _L0_attn_in['u'], 'L0_ffn_gate_W': _L0_ffn_in['gate_W'], 'L0_ffn_w1_e': _L0_ffn_in['w1_e'], 'L0_ffn_w3_e': _L0_ffn_in['w3_e'], 'L0_ffn_w2_e': _L0_ffn_in['w2_e'], 'L0_ffn_w1_s': _L0_ffn_in['w1_s'], 'L0_ffn_w3_s': _L0_ffn_in['w3_s'], 'L0_ffn_w2_s': _L0_ffn_in['w2_s']}
    _x0 = _d['L0_attn_x']
    _d['L0_attn_x'] = jax.random.normal(jax.random.fold_in(jax.random.key(seed), 1), (16, 512, 128), dtype=_x0.dtype)
    del _x0
    return _d

def reference(L0_attn_x, L0_attn_Wr, L0_attn_Wk, L0_attn_Wv, L0_attn_Wo, L0_attn_r_mu, L0_attn_k_mu, L0_attn_v_mu, L0_attn_w, L0_attn_u, L0_ffn_gate_W, L0_ffn_w1_e, L0_ffn_w3_e, L0_ffn_w2_e, L0_ffn_w1_s, L0_ffn_w3_s, L0_ffn_w2_s):

    def _L0_attn_ref(x, Wr, Wk, Wv, Wo, r_mu, k_mu, v_mu, w, u):
        import jax, jax.numpy as jnp
        import numpy as np
        DIM = 128
        B, T = (8, 128)

        def _wkv(w, u, k, v):
            e_dec = jnp.exp(-w)
            e_grow = jnp.exp(w)
            Tlen = k.shape[1]
            cnt = jnp.maximum(jnp.arange(Tlen) - 1, 0).astype(k.dtype)
            msk = (jnp.arange(Tlen) > 0).astype(k.dtype)

            def step(carry, inp):
                A, Bacc = carry
                kt, vt, ct, mt = inp
                out = A + jnp.exp(u + kt) * (vt * Bacc + ct)
                ek = jnp.exp(kt)
                A = e_dec * A + mt * ek * vt
                Bacc = e_grow * Bacc + mt / ek
                return ((A, Bacc), out)
            kT = jnp.moveaxis(k, 1, 0)
            vT = jnp.moveaxis(v, 1, 0)
            z = jnp.zeros_like(k[:, 0])
            _, outs = jax.lax.scan(step, (z, z), (kT, vT, cnt, msk))
            return jnp.moveaxis(outs, 0, 1)
        x1 = jnp.pad(x, ((0, 0), (1, 0), (0, 0)))[:, :-1, :]
        r = jnp.einsum('btd,od->bto', x * r_mu + x1 * (1.0 - r_mu), Wr)
        k = jnp.einsum('btd,od->bto', x * k_mu + x1 * (1.0 - k_mu), Wk)
        v = jnp.einsum('btd,od->bto', x * v_mu + x1 * (1.0 - v_mu), Wv)
        wkv = _wkv(w, u, k, v)
        return jnp.einsum('btd,od->bto', jax.nn.sigmoid(r) * wkv, Wo)

    def _L0_ffn_ref(hidden_states, gate_W, w1_e, w3_e, w2_e, w1_s, w3_s, w2_s):
        import jax, jax.numpy as jnp
        import numpy as np
        B, S, D, F, E, NS, K = (2, 128, 128, 512, 8, 8, 2)
        FS = F // NS
        b, s, d = hidden_states.shape
        e = gate_W.shape[0]
        flat = hidden_states.reshape(-1, d)
        T = flat.shape[0]
        logits = (flat @ gate_W.T).astype(jnp.float32)
        probs = jax.nn.softmax(logits, axis=-1)
        top_v, top_i = jax.lax.top_k(probs, K)
        gates = jnp.zeros((T, e), probs.dtype).at[jnp.arange(T)[:, None], top_i].set(top_v)
        g = jax.nn.silu(jnp.einsum('td,edf->etf', flat, w1_e))
        u = jnp.einsum('td,edf->etf', flat, w3_e)
        out_e = jnp.einsum('etf,efd->etd', g * u, w2_e)
        routed = jnp.einsum('te,etd->td', gates, out_e).reshape(b, s, d)
        gs = jax.nn.silu(jnp.einsum('bsd,ndf->nbsf', hidden_states, w1_s))
        us = jnp.einsum('bsd,ndf->nbsf', hidden_states, w3_s)
        shared = jnp.einsum('nbsf,nfd->bsd', gs * us, w2_s) / w1_s.shape[0]
        alpha = 0.5
        return alpha * shared + (1.0 - alpha) * routed
    x = L0_attn_x
    x = x + _layernorm(_L0_attn_ref(_layernorm(x, axis=-1), L0_attn_Wr, L0_attn_Wk, L0_attn_Wv, L0_attn_Wo, L0_attn_r_mu, L0_attn_k_mu, L0_attn_v_mu, L0_attn_w, L0_attn_u), axis=-1)
    x = x + _layernorm(_L0_ffn_ref(_layernorm(x, axis=-1), L0_ffn_gate_W, L0_ffn_w1_e, L0_ffn_w3_e, L0_ffn_w2_e, L0_ffn_w1_s, L0_ffn_w3_s, L0_ffn_w2_s), axis=-1)
    return x

_drawn_inputs = setup_inputs


def setup_inputs(seed=0):
    import zlib

    import numpy as np

    out = dict(_drawn_inputs(seed))
    spreads = {}
    factors = {}
    for name, (base, spread) in spreads.items():
        noise = np.random.default_rng([zlib.crc32(name.encode()), seed]).standard_normal(out[name].shape)
        drawn = base * np.exp(spread * noise) if base else spread * noise
        out[name] = jnp.asarray(drawn.astype(out[name].dtype))
    for name, factor in factors.items():
        out[name] = (out[name] * factor).astype(out[name].dtype)
    return out
```

```python
from contextlib import ExitStack

import concourse.bass as bass
from concourse import mybir

F32 = mybir.dt.float32
BF16 = mybir.dt.bfloat16
I32 = mybir.dt.int32
ALU = mybir.AluOpType
ACT = mybir.ActivationFunctionType
AX_X = mybir.AxisListType.X

P = 128
EPS = 1e-5
LOWEST = -3.0e38


def wait(eng, sem, value):
    if isinstance(value, int) and value <= 0:
        return
    eng.wait_ge(sem, value)


class Own:

    def __init__(self, eng, sem, per, step, passed=None):
        self.eng, self.sem, self.per, self.base, self.n, self.passed = eng, sem, per, step * per, 0, passed

    def did(self, ins):
        self.n += 1
        ins.then_inc(self.sem, 1)

    def settle(self):
        self.eng.wait_ge(self.sem, self.base + self.n)
        if self.passed is not None:
            self.eng.sem_inc(self.passed, 1)

    def end(self):
        assert self.n == self.per, (self.n, self.per)


def pipeline(eng, count, skew, step):
    first, last = skew + skew % 2 + 2, count - count % 2
    for t in range(first):
        step(t, t % 2)
    with eng.Fori(0, (last - first) // 2) as i:
        for par in range(2):
            step(2 * i + (first + par), par)
    for t in range(last, count + skew):
        step(t, t % 2)


def within(t, count):
    return not isinstance(t, int) or 0 <= t < count


def build(nc, x_d, Wr_d, Wk_d, Wv_d, Wo_d, rmu_d, kmu_d, vmu_d, w_d, u_d,
          gate_d, w1_d, w3_d, w2_d, w1s_d, w3s_d, w2s_d, out_d):
    NB, T, D = x_d.shape
    E, _, F = w1_d.shape
    NS, _, FS = w1s_d.shape
    J = T // P
    C = F // P
    SEL = 2
    TOK = NB * T
    assert D == P and NS * FS == F and NB % 2 == 0 and T == 512
    REGION = TOK + P
    SLOTS = SEL * TOK // P + E
    ROWS = E * REGION + E * P

    x_t = x_d.rearrange("b (j p) d -> b p j d", p=P)
    out_t = out_d.rearrange("b (j p) d -> b p j d", p=P)

    xs_d = nc.dram_tensor("xs_rows", [ROWS, D], F32, kind="Internal").ap()
    ys_d = nc.dram_tensor("ys_rows", [SLOTS * P, D], F32, kind="Internal").ap()
    xfT_d = nc.dram_tensor("xfT_batches", [NB * P, T], F32, kind="Internal").ap()

    with ExitStack() as ctx:
        def sb(name, shape, dt=F32):
            return ctx.enter_context(nc.sbuf_tensor(name, shape, dt))

        def sem(name):
            return ctx.enter_context(nc.semaphore(name))

        def sem2(name):
            return [sem(name + "_even"), sem(name + "_odd")]

        bank = [ctx.enter_context(nc.psum_tensor(f"bank{n}", [P, 512], F32)) for n in range(8)]

        w1 = sb("w1", [P, E, F])
        w3 = sb("w3", [P, E, F])
        w2 = sb("w2", [P, E, C, D])
        w1s = sb("w1s", [P, NS, FS])
        w3s = sb("w3s", [P, NS, FS])
        w2s = sb("w2s", [P, C, D])
        raw = sb("raw", [P, 4, P])
        gate_raw = sb("gate_raw", [E, P])
        mix_w = sb("mix_w", [P, 3, 2, P])
        woT = sb("woT", [P, P])
        gateT = sb("gateT", [P, E])
        mu = sb("mu", [P, 3])
        omu = sb("omu", [P, 3])
        wvec = sb("wvec", [P, 1])
        uvec = sb("uvec", [P, 1])
        eu = sb("eu", [P, 1])
        decay = sb("decay", [P, T])
        grow = sb("grow", [P, T])
        wfull = sb("wfull", [P, T])
        ident = sb("ident", [P, P])
        upper = sb("upper", [P, P], BF16)
        ones = sb("ones", [P, P], BF16)
        zrow = sb("zrow", [P, P])
        first = sb("first", [P, J, E])
        cnt = sb("cnt", [P, T])
        mhalf = sb("mhalf", [P, J])

        x_all = sb("x_all", [P, NB, J * D])
        pos_all = sb("pos_all", [P, NB * 8])
        ypos = sb("ypos", [P, NB * 8])
        ypos_i = sb("ypos_i", [P, NB * 8], I32)
        gates_all = sb("gates_all", [P, NB * 8])

        xn = sb("xn", [P, J, D])
        xT = sb("xT", [P, 2, T + 2])
        ek = sb("ek", [P, 2, T])
        enk = sb("enk", [P, 2, T])
        th = sb("th", [P, 2, T])
        ekv = sb("ekv", [P, T])
        Aprev = sb("Aprev", [P, T])
        Bprev = sb("Bprev", [P, T])
        ekcnt = sb("ekcnt", [P, 2, T])
        vb = sb("vb", [P, T])
        vbc = sb("vbc", [P, T])
        wkv = sb("wkv", [P, T])
        y = sb("y", [P, 2, T])
        an = sb("an", [P, J, D])
        xf = sb("xf", [P, 2, J, D])
        xfT = sb("xfT", [P, 2, T])
        stats = [sb(f"stats{n}", [P, J, 6]) for n in range(3)]
        mv = [sb(f"mv{n}", [P, J, 2]) for n in range(3)]
        veps = [sb(f"veps{n}", [P, J]) for n in range(3)]
        rstd = [sb(f"rstd{n}", [P, J]) for n in range(3)]

        lmax = sb("lmax", [P, J])
        ldiff = sb("ldiff", [P, J, E])
        expl = sb("expl", [P, 2, J * E])
        cand = sb("cand", [P, J, E])
        cbest = sb("cbest", [P, J])
        rest = sb("rest", [P, J, E])
        rmax = sb("rmax", [P, J])
        cand2 = sb("cand2", [P, J, E])
        cand3 = sb("cand3", [P, J, E])
        cbest2 = sb("cbest2", [P, J])
        chosen = sb("chosen", [P, SEL, J * E])
        both = sb("both", [P, J * E], BF16)
        nextrow = sb("nextrow", [P, E])
        gap = sb("gap", [P, NB * 8])
        rank = sb("rank", [P, J, E])
        picked = sb("picked", [P, SEL * J, E])
        posf = sb("posf", [P, SEL * J])
        idx = sb("idx", [P, 2, SEL * J], I32)
        pickedg = sb("pickedg", [P, SEL * J, E])
        gsum = sb("gsum", [P, SEL, J])
        zsum = sb("zsum", [P, J])
        zinv = sb("zinv", [P, J])

        padrow = sb("padrow", [P, E])
        padidx = sb("padidx", [P, E], I32)
        lane = sb("lane", [P, 1])
        region0 = sb("region0", [P, E])
        tcount = sb("tcount", [P, E])
        tedge = sb("tedge", [P, E, TOK // P])
        tnum = sb("tnum", [P, E])
        tend = sb("tend", [P, E])
        tjump = sb("tjump", [P, E])
        one8 = sb("one8", [P, E])
        slotno = sb("slotno", [1, SLOTS])
        edge0 = sb("edge0", [P, TOK // P])
        past = sb("past", [1, E, SLOTS])
        pastj = sb("pastj", [1, E, SLOTS])
        slot_e = sb("slot_e", [1, SLOTS])
        slot_r = sb("slot_r", [1, SLOTS])
        slot_w = sb("slot_w", [1, SLOTS], I32)
        slot_row = sb("slot_row", [1, SLOTS], I32)

        xs = sb("xs", [P, 2, D])
        xsT = sb("xsT", [P, 2, P])
        sg = sb("sg", [P, F])
        h = sb("h", [P, 2, F])
        hT = sb("hT", [P, 2, F])
        ys = sb("ys", [P, 2, D])

        consts, consts2 = sem("consts"), sem("consts2")
        w_small, w_big = sem("w_small"), sem("w_big")
        turned, setup_act, setup_dve = sem("turned"), sem("setup_act"), sem("setup_dve")
        x_in = sem2("x_in")
        ln_stats = [sem(f"ln{n}_stats") for n in range(3)]
        ln_rstd = [sem(f"ln{n}_rstd") for n in range(3)]
        xn_ready, xT_psum, xT_ready = sem("xn_ready"), sem("xT_psum"), sem("xT_ready")
        rkv_psum, exps_ready = sem("rkv_psum"), sem("exps_ready")
        ekcnt_ready, y_ready = sem("ekcnt_ready"), sem("y_ready")
        attn_psum = sem("attn_psum")
        xf_ready, xfT_psum, xfT_ready = sem("xf_ready"), sem("xfT_psum"), sem("xfT_ready")
        xfT_out = sem2("xfT_out")
        logits_psum, ldiff_ready, expl_ready = sem("logits_psum"), sem("ldiff_ready"), sem("expl_ready")
        both_ready, rank_psum, idx_ready = sem("both_ready"), sem("rank_psum"), sem("idx_ready")
        scattered = sem2("scattered")
        own = {k: sem("own_" + k) for k in ("d0", "c0", "c1", "d2", "d3", "d4", "d6", "d7", "p0", "p1", "p2", "dc", "dd", "dg", "pt")}
        passed, dve_passed = sem("pool_passed"), sem("dve_passed")
        pads_ready, padded, table_ready = sem("pads_ready"), sem("padded"), sem("table_ready")
        ypos_ready = sem("ypos_ready")
        xs_in = sem2("xs_in")
        xsT_psum, xsT_ready = sem("xsT_psum"), sem("xsT_ready")
        g_psum, u_psum, silu_ready, h_ready = sem("g_psum"), sem("u_psum"), sem("silu_ready"), sem("h_ready")
        hT_psum, hT_ready, y_psum, ys_ready = sem("hT_psum"), sem("hT_ready"), sem("y_psum"), sem("ys_ready")
        ys_out = sem2("ys_out")
        f_in = sem2("f_in")
        fgu_psum, fsilu, fh_ready = sem("fgu_psum"), sem("fsilu"), sem("fh_ready")
        shared_psum, shared_used = sem("shared_psum"), sem("shared_used")
        gidx_ready = sem("gidx_ready")
        gathered = sem2("gathered")
        fstats, frstd, res_ready = sem("fstats"), sem("frstd"), sem("res_ready")
        out_done = sem2("out_done")

        block = ctx.enter_context(nc.Block())

        ps_xT, ps_xfT, ps_r, ps_k, ps_attn, ps_small = (bank[n] for n in (0, 1, 2, 3, 6, 7))
        ps_v = (bank[4], bank[5])
        ps_logits = ps_small[:, 0:J * E]
        ps_rank = ps_small[:, J * E:2 * J * E]
        ps_total = ps_small[:, 2 * J * E:2 * J * E + E]
        ps_xsT, ps_g, ps_u, ps_hT, ps_y = (bank[n] for n in (0, 1, 2, 3, 4))
        ps_fg, ps_fu, ps_sh = bank[0:2], bank[2:4], bank[4:6]

        def xcols(b):
            v = x_all[:, b, :] if isinstance(b, int) else x_all[:, bass.ds(b, 1), :].rearrange("p a n -> p (a n)")
            return v.rearrange("p (j d) -> p j d", d=D)

        fxT = xfT
        fsg = ek
        fh = enk
        gath = [sb(f"gath{n}", [P, SEL * J, D]) for n in range(2)]
        gidx = sb("gidx", [P, 2, SEL * J], I32)
        acc = sb("acc", [P, J, D])
        acc2 = sb("acc2", [P, J, D])
        fst = sb("fst", [P, J, 6])
        fmv = sb("fmv", [P, J, 2])
        fve = sb("fve", [P, J])
        frs = sb("frs", [P, J])
        fn = sb("fn", [P, J, D])
        res = sb("res", [P, 2, J, D])

        @block.sync
        def _(sp):
            for n, wd in enumerate((Wr_d, Wk_d, Wv_d, Wo_d)):
                sp.dma_start(raw[:, n, :], wd).then_inc(w_small, 16)
            sp.dma_start(gate_raw[:, :], gate_d).then_inc(w_small, 16)
            for n, vd in enumerate((rmu_d, kmu_d, vmu_d)):
                sp.dma_start(mu[:, n:n + 1], vd.rearrange("(d a) -> d a", a=1)).then_inc(w_small, 16)
            sp.dma_start(wvec[:, :], w_d.rearrange("(d a) -> d a", a=1)).then_inc(w_small, 16)
            sp.dma_start(uvec[:, :], u_d.rearrange("(d a) -> d a", a=1)).then_inc(w_small, 16)
            for b in range(2):
                sp.dma_start(xcols(b), x_t[b]).then_inc(x_in[b], 16)
            sp.dma_start(w1[:, :, :], w1_d.rearrange("e d f -> d e f")).then_inc(w_big, 16)
            sp.dma_start(w3[:, :, :], w3_d.rearrange("e d f -> d e f")).then_inc(w_big, 16)
            sp.dma_start(w2[:, :, :, :], w2_d.rearrange("e (c f) d -> f e c d", f=P)).then_inc(w_big, 16)
            sp.dma_start(w1s[:, :, :], w1s_d.rearrange("n d f -> d n f")).then_inc(w_big, 16)
            sp.dma_start(w3s[:, :, :], w3s_d.rearrange("n d f -> d n f")).then_inc(w_big, 16)
            sp.dma_start(w2s[:, :, :], w2s_d.rearrange("n f d -> (n f) d").rearrange("(c f) d -> f c d", f=P)).then_inc(w_big, 16)

            for b in range(2, NB):
                sp.wait_ge(x_in[b % 2], 16 * (b // 2))
                sp.dma_start(xcols(b), x_t[b]).then_inc(x_in[b % 2], 16)

            with sp.Fori(0, NB // 2) as i:
                for par in range(2):
                    sp.wait_ge(xfT_ready, 2 * i + (par + 1))
                    sp.dma_start(xfT_d[bass.ds((2 * i + par) * P, P), :], xfT[:, par, :]).then_inc(xfT_out[par], 16)

            sp.wait_ge(table_ready, 1)
            for q in range(2):
                sp.wait_ge(scattered[q], NB // 2 * SEL * J * 16)
            sp.wait_ge(padded, (E + 1) * 16)

            def move(s, par):
                if within(s, SLOTS):
                    wait(sp, xsT_psum, s - 1)
                    row = sp.value_load(slot_row[0:1, s:s + 1] if isinstance(s, int) else slot_row[0:1, bass.ds(s, 1)],
                                        min_val=0, max_val=ROWS - P)
                    sp.dma_start(xs[:, par, :], xs_d[bass.ds(row, P), :]).then_inc(xs_in[par], 16)
                if within(s - 3, SLOTS):
                    sp.wait_ge(ys_ready, s - 2)
                    o = s - 3
                    sp.dma_start(ys_d[o * P:(o + 1) * P, :] if isinstance(o, int) else ys_d[bass.ds(o * P, P), :], ys[:, (par + 1) % 2, :]).then_inc(ys_out[(par + 1) % 2], 16)

            pipeline(sp, SLOTS, 3, move)

            def carry(b, par):
                if within(b, NB):
                    if isinstance(b, int) and b < 2:
                        sp.wait_ge(xfT_out[par], NB // 2 * 16)
                    wait(sp, fgu_psum, C * (b - 1))
                    sp.dma_start(fxT[:, par, :], xfT_d[b * P:(b + 1) * P, :] if isinstance(b, int)
                                 else xfT_d[bass.ds(b * P, P), :]).then_inc(f_in[par], 16)
                if within(b - 2, NB):
                    o = b - 2
                    sp.wait_ge(res_ready, b - 1)
                    dst = out_t[o] if isinstance(o, int) else out_t[bass.ds(o, 1)].rearrange("a p j d -> p (a j) d")
                    sp.dma_start(dst, res[:, par, :, :]).then_inc(out_done[par], 16)

            pipeline(sp, NB, 2, carry)
            for q in range(2):
                sp.wait_ge(out_done[q], NB // 2 * 16)

        @block.gpsimd
        def _(pool):
            g = nc.gpsimd
            g.memset(ident[:, :], 0.0).then_inc(consts2, 1)
            g.memset(upper[:, :], 0.0).then_inc(consts2, 1)
            g.memset(ones[:, :], 1.0).then_inc(consts, 1)
            g.memset(zrow[:, :], 0.0).then_inc(consts, 1)
            g.memset(mhalf[:, :], -0.5).then_inc(consts, 1)
            g.memset(one8[:, :], 1.0).then_inc(consts, 1)
            g.memset(xT[:, 0, 0:2], 0.0).then_inc(consts, 1)
            g.memset(xT[:, 1, 0:2], 0.0).then_inc(consts, 1)
            g.memset(Aprev[:, 0:2], 0.0).then_inc(consts, 1)
            g.memset(Bprev[:, 0:2], 0.0).then_inc(consts, 1)
            g.iota(first[:, :, :], pattern=[[0, J], [-1, E]], base=E, channel_multiplier=0,
                   allow_small_or_imprecise_dtypes=True).then_inc(consts, 1)
            g.iota(cnt[:, 1:T], pattern=[[1, T - 1]], base=0, channel_multiplier=0,
                   allow_small_or_imprecise_dtypes=True).then_inc(consts, 1)
            g.memset(cnt[:, 0:1], 0.0).then_inc(consts, 1)
            g.iota(nextrow[:, :], pattern=[[REGION, E]], base=0, channel_multiplier=0,
                   allow_small_or_imprecise_dtypes=True).then_inc(consts, 1)
            g.iota(region0[:, :], pattern=[[REGION, E]], base=0, channel_multiplier=0,
                   allow_small_or_imprecise_dtypes=True).then_inc(consts, 1)
            g.iota(lane[:, :], pattern=[[0, 1]], base=0, channel_multiplier=1,
                   allow_small_or_imprecise_dtypes=True).then_inc(consts, 1)
            g.iota(slotno[:, :], pattern=[[1, SLOTS]], base=0, channel_multiplier=0,
                   allow_small_or_imprecise_dtypes=True).then_inc(consts, 1)
            g.iota(edge0[:, :], pattern=[[P, TOK // P]], base=0, channel_multiplier=0,
                   allow_small_or_imprecise_dtypes=True).then_inc(consts, 1)
            pool.wait_ge(consts2, 2)
            g.affine_select(out=ident[:, :], in_=ident[:, :], compare_op=ALU.not_equal, fill=1.0, base=0,
                            pattern=[[-1, P]], channel_multiplier=1).then_inc(consts, 1)
            g.affine_select(out=upper[:, :], in_=upper[:, :], compare_op=ALU.is_ge, fill=1.0, base=0,
                            pattern=[[-1, P]], channel_multiplier=1).then_inc(consts, 1)
            pool.wait_ge(consts, 18)

            def rsqrt(n, b, key):
                me = Own(pool, own[key], 1, b, passed)
                pool.wait_ge(ln_stats[n], b + 1)
                pool.sem_inc(passed, 1)
                me.did(g.tensor_scalar(veps[n][:, :], mv[n][:, :, 1], EPS, None, ALU.add))
                me.settle()
                g.tensor_tensor(rstd[n][:, :], veps[n][:, :], mhalf[:, :], ALU.pow).then_inc(ln_rstd[n], 1)
                me.end()

            def step(t, par):
                if within(t, NB):
                    rsqrt(0, t, "p0")
                if within(t - 1, NB):
                    b, q = t - 1, 1 - par
                    pool.wait_ge(exps_ready, t)
                    pool.sem_inc(passed, 1)
                    wait(pool, y_ready, t - 2)
                    pool.sem_inc(passed, 1)
                    g.tensor_tensor(ekcnt[:, q, :], ek[:, q, :], cnt[:, :], ALU.mult).then_inc(ekcnt_ready, 1)
                    rsqrt(1, b, "p1")
                    rsqrt(2, b, "p2")
                if within(t - 2, NB):
                    pool.wait_ge(idx_ready, t - 1)
                    pool.sem_inc(passed, 1)
                    for k in range(SEL):
                        for j in range(J):
                            pool.indirect_dma_start(
                                xs_d[:, :], bass.IndirectOffsetOnAxis(ap=idx[:, par, k * J + j:k * J + j + 1], axis=0),
                                xf[:, par, j, :], None).then_inc(scattered[par], 16)

            pipeline(pool, NB, 2, step)

            pool.wait_ge(pads_ready, 1)
            for e in range(E):
                pool.indirect_dma_start(xs_d[:, :], bass.IndirectOffsetOnAxis(ap=padidx[:, e:e + 1], axis=0),
                                        zrow[:, :], None).then_inc(padded, 16)
            pool.dma_start(xs_d[E * REGION:ROWS, :].rearrange("(a p) d -> p a d", p=P),
                           zrow[:, :].rearrange("p (a d) -> p a d", a=1).to_broadcast([P, E, D])).then_inc(padded, 16)

            pool.wait_ge(ypos_ready, 1)
            for q in range(2):
                pool.wait_ge(ys_out[q], SLOTS // 2 * 16)

            def gather(b, par):
                if within(b, NB):
                    wait(pool, shared_used, b - 1)
                    pool.sem_inc(passed, 1)
                    src = ypos_i[:, b * 8:(b + 1) * 8] if isinstance(b, int) else ypos_i[:, bass.ds(b * 8, 8)]
                    wait(pool, gathered[par], 8 * 8 * (b - par))
                    pool.sem_inc(passed, 1)
                    g.tensor_copy(gidx[:, par, :], src).then_inc(gidx_ready, 1)
                    pool.wait_ge(gidx_ready, b + 1)
                    pool.sem_inc(passed, 1)
                    for n in range(SEL * J):
                        pool.indirect_dma_start(
                            gath[par][:, n, :], None, ys_d[:, :],
                            bass.IndirectOffsetOnAxis(ap=gidx[:, par, n:n + 1], axis=0)).then_inc(gathered[par], 16)
                if within(b - 1, NB):
                    me = Own(pool, own["pt"], 1, b - 1, passed)
                    pool.wait_ge(fstats, b)
                    pool.sem_inc(passed, 1)
                    me.did(g.tensor_scalar(fve[:, :], fmv[:, :, 1], EPS, None, ALU.add))
                    me.settle()
                    g.tensor_tensor(frs[:, :], fve[:, :], mhalf[:, :], ALU.pow).then_inc(frstd, 1)

            pipeline(pool, NB, 1, gather)

        @block.scalar
        def _(act):
            s = nc.scalar
            act.wait_ge(w_small, 160)
            s.activation(eu[:, :], uvec[:, :], ACT.Exp).then_inc(setup_act, 1)
            act.wait_ge(setup_dve, 2)
            s.activation(decay[:, :], wfull[:, :], ACT.Exp, scale=-1.0).then_inc(setup_act, 1)
            s.activation(grow[:, :], wfull[:, :], ACT.Exp).then_inc(setup_act, 1)

            def step(t, par):
                if within(t - 2, NB):
                    act.wait_ge(xfT_psum, t - 1)
                    wait(act, logits_psum, t - 3)
                    if not isinstance(t, int):
                        act.wait_ge(xfT_out[par], 8 * (t - 2 - par))
                    elif t - 2 >= 2:
                        act.wait_ge(xfT_out[par], 16 * ((t - 2) // 2))
                    s.activation(xfT[:, par, :], ps_xfT[:, :], ACT.Copy).then_inc(xfT_ready, 1)
                if within(t, NB):
                    act.wait_ge(xT_psum, t + 1)
                    wait(act, rkv_psum, t - 1)
                    s.activation(xT[:, par, 2:T + 2], ps_xT[:, :], ACT.Copy).then_inc(xT_ready, 1)
                if within(t - 2, NB):
                    act.wait_ge(ldiff_ready, t - 1)
                    s.activation(expl[:, par, :], ldiff[:, :, :].rearrange("p j e -> p (j e)"), ACT.Exp)\
                     .then_inc(expl_ready, 1)
                if within(t, NB):
                    act.wait_ge(rkv_psum, t + 1)
                    wait(act, y_ready, t - 1)
                    s.activation(th[:, par, :], ps_r[:, :], ACT.Tanh, scale=0.5)
                    s.activation(enk[:, par, :], ps_k[:, :], ACT.Exp, scale=-1.0)
                    s.activation(ek[:, par, :], ps_k[:, :], ACT.Exp).then_inc(exps_ready, 1)

            pipeline(act, NB, 2, step)

            def tile(k, par):
                if within(k, SLOTS):
                    act.wait_ge(xsT_psum, k + 1)
                    wait(act, u_psum, k - 1)
                    s.activation(xsT[:, par, :], ps_xsT[:, 0:P], ACT.Copy).then_inc(xsT_ready, 1)
                if within(k - 1, SLOTS):
                    act.wait_ge(g_psum, k)
                    wait(act, h_ready, k - 1)
                    s.activation(sg[:, :], ps_g[:, :], ACT.Silu).then_inc(silu_ready, 1)
                if within(k - 2, SLOTS):
                    act.wait_ge(hT_psum, k - 1)
                    wait(act, y_psum, k - 3)
                    s.activation(hT[:, par, :], ps_hT[:, :], ACT.Copy).then_inc(hT_ready, 1)

            pipeline(act, SLOTS, 2, tile)

            def shared(b, par):
                for c in range(C if within(b, NB) else 0):
                    act.wait_ge(fgu_psum, C * b + (c + 1))
                    wait(act, fh_ready, C * b + (c - 1))
                    s.activation(fsg[:, c % 2, :], ps_fg[c % 2][:, :], ACT.Silu).then_inc(fsilu, 1)

            pipeline(act, NB, 0, shared)

        @block.tensor
        def _(pe):
            p = nc.tensor
            pe.wait_ge(w_small, 160)
            pe.wait_ge(consts, 18)
            for n in range(4):
                p.transpose(bank[0][:, n * P:(n + 1) * P], raw[:, n, :], ident[:, :])
            p.transpose(bank[1][:, 0:E], gate_raw[:, :], ident[0:E, 0:E]).then_inc(turned, 1)
            pe.wait_ge(setup_dve, 11)

            def step(t, par):
                if within(t - 2, NB):
                    b = t - 2
                    pe.wait_ge(xf_ready, t - 1)
                    wait(pe, xfT_ready, t - 2)
                    for j in range(J):
                        last = p.transpose(ps_xfT[:, j * P:(j + 1) * P], xf[:, par, j, :], ident[:, :])
                    last.then_inc(xfT_psum, 1)
                if within(t, NB):
                    pe.wait_ge(xn_ready, t + 1)
                    wait(pe, xT_ready, t)
                    for j in range(J):
                        last = p.transpose(ps_xT[:, j * P:(j + 1) * P], xn[:, j, :], ident[:, :])
                    last.then_inc(xT_psum, 1)
                if within(t - 2, NB):
                    pe.wait_ge(xfT_ready, t - 1)
                    wait(pe, idx_ready, t - 2)
                    for j in range(J):
                        last = p.matmul(ps_logits[:, j * E:(j + 1) * E], xfT[:, par, j * P:(j + 1) * P], gateT[:, :],
                                        start=True, stop=True)
                    last.then_inc(logits_psum, 1)
                if within(t, NB):
                    pe.wait_ge(xT_ready, t + 1)
                    wait(pe, exps_ready, t)
                    wait(pe, y_ready, t - 1)
                    for n, dst in enumerate((ps_r, ps_k, ps_v[par])):
                        p.matmul(dst[:, :], mix_w[:, n, 0, :], xT[:, par, 2:T + 2], start=True, stop=False)
                        last = p.matmul(dst[:, :], mix_w[:, n, 1, :], xT[:, par, 1:T + 1], start=False, stop=True)
                    last.then_inc(rkv_psum, 1)
                if within(t - 1, NB):
                    pe.wait_ge(y_ready, t)
                    wait(pe, ln_stats[2], t - 1)
                    for j in range(J):
                        last = p.matmul(ps_attn[:, j * P:(j + 1) * P], y[:, 1 - par, j * P:(j + 1) * P], woT[:, :],
                                        start=True, stop=True)
                    last.then_inc(attn_psum, 1)
                if within(t - 2, NB):
                    pe.wait_ge(both_ready, t - 1)
                    p.matmul(ps_rank, upper[:, :], both[:, :], start=True, stop=False)
                    for j in range(1, J):
                        p.matmul(ps_rank[:, j * E:J * E], ones[:, :], both[:, 0:(J - j) * E], start=False, stop=(j == J - 1))
                    for j in range(J):
                        last = p.matmul(ps_total, ones[:, :], both[:, j * E:(j + 1) * E], start=(j == 0), stop=(j == J - 1))
                    last.then_inc(rank_psum, 1)

            pipeline(pe, NB, 2, step)

            pe.wait_ge(w_big, 96)
            pe.wait_ge(table_ready, 1)

            def offset(k):
                return pe.value_load(slot_w[0:1, k:k + 1] if isinstance(k, int) else slot_w[0:1, bass.ds(k, 1)],
                                     min_val=0, max_val=(E - 1) * F)

            w1f = w1[:, :, :].rearrange("p e f -> p (e f)")
            w3f = w3[:, :, :].rearrange("p e f -> p (e f)")
            w2f = w2[:, :, :, :].rearrange("p e c d -> p (e c d)")

            def tile(k, par):
                if within(k, SLOTS):
                    pe.wait_ge(xs_in[par], 16 * (k // 2) + 16 if isinstance(k, int) else 8 * (k - par) + 16)
                    wait(pe, xsT_ready, k)
                    p.transpose(ps_xsT[:, 0:P], xs[:, par, :], ident[:, :]).then_inc(xsT_psum, 1)
                if within(k - 1, SLOTS):
                    e = offset(k - 1)
                    pe.wait_ge(xsT_ready, k)
                    wait(pe, silu_ready, k - 1)
                    p.matmul(ps_g[:, :], xsT[:, 1 - par, :], w1f[:, bass.ds(e, F)], start=True, stop=True).then_inc(g_psum, 1)
                if within(k - 2, SLOTS):
                    pe.wait_ge(h_ready, k - 1)
                    wait(pe, hT_ready, k - 2)
                    for c in range(C):
                        last = p.transpose(ps_hT[:, c * P:(c + 1) * P], h[:, par, c * P:(c + 1) * P], ident[:, :])
                    last.then_inc(hT_psum, 1)
                if within(k - 1, SLOTS):
                    wait(pe, h_ready, k - 1)
                    p.matmul(ps_u[:, :], xsT[:, 1 - par, :], w3f[:, bass.ds(e, F)], start=True, stop=True).then_inc(u_psum, 1)
                if within(k - 2, SLOTS):
                    e2 = offset(k - 2)
                    pe.wait_ge(hT_ready, k - 1)
                    wait(pe, ys_ready, k - 2)
                    for c in range(C):
                        last = p.matmul(ps_y[:, 0:D], hT[:, par, c * P:(c + 1) * P], w2f[:, bass.ds(e2 + c * D, D)],
                                        start=(c == 0), stop=(c == C - 1))
                    last.then_inc(y_psum, 1)

            pipeline(pe, SLOTS, 2, tile)

            def pair(b, par):
                if not within(b, NB):
                    return
                pe.wait_ge(f_in[par], 16 * (b // 2) + 16 if isinstance(b, int) else 8 * (b - par) + 16)

                def up(c):
                    wait(pe, fh_ready, C * b + (c - 1))
                    for dst, w in ((ps_fg, w1s), (ps_fu, w3s)):
                        wf = w[:, :, :].rearrange("p n f -> p (n f)")
                        last = p.matmul(dst[c % 2][:, :], wf[:, c * P:(c + 1) * P], fxT[:, par, :], start=True, stop=True)
                    last.then_inc(fgu_psum, 1)

                def down(c):
                    pe.wait_ge(fh_ready, C * b + (c + 1))
                    if c == 0:
                        wait(pe, shared_used, b - 1)
                    for j in range(J):
                        last = p.matmul(ps_sh[par][:, j * P:(j + 1) * P], fh[:, c % 2, j * P:(j + 1) * P], w2s[:, c, :],
                                        start=(c == 0 and j == 0), stop=(c == C - 1), skip_group_check=True)
                    if c == C - 1:
                        last.then_inc(shared_psum, 1)

                up(0)
                for c in range(1, C):
                    up(c)
                    down(c - 1)
                down(C - 1)

            pipeline(pe, NB, 0, pair)

        @block.vector
        def _(dve):
            v = nc.vector
            dve.wait_ge(w_small, 160)
            dve.wait_ge(consts, 18)
            v.memset(wfull[:, :], 0.0).then_inc(setup_dve, 1)
            dve.wait_ge(setup_dve, 1)
            v.tensor_scalar(wfull[:, :], wfull[:, :], wvec[:, 0:1], None, ALU.add).then_inc(setup_dve, 1)
            v.tensor_scalar(omu[:, :], mu[:, :], -1.0, 1.0, ALU.mult, ALU.add).then_inc(setup_dve, 1)
            dve.wait_ge(setup_dve, 3)
            dve.wait_ge(turned, 1)
            for n in range(3):
                src = bank[0][:, n * P:(n + 1) * P]
                v.tensor_scalar(mix_w[:, n, 0, :], src, mu[:, n:n + 1], None, ALU.mult).then_inc(setup_dve, 1)
                v.tensor_scalar(mix_w[:, n, 1, :], src, omu[:, n:n + 1], None, ALU.mult).then_inc(setup_dve, 1)
            v.tensor_scalar(woT[:, :], bank[0][:, 3 * P:4 * P], 0.5, None, ALU.mult).then_inc(setup_dve, 1)
            v.tensor_copy(gateT[:, :], bank[1][:, 0:E]).then_inc(setup_dve, 1)
            dve.wait_ge(w_big, 96)
            v.tensor_scalar(w2s[:, :, :], w2s[:, :, :], 0.5 / NS, None, ALU.mult).then_inc(setup_dve, 1)
            dve.wait_ge(setup_act, 3)

            def ln(me, n, src):
                dve.sem_inc(dve_passed, 1)
                for j in range(J):
                    me.did(v.bn_stats(stats[n][:, j, :], src[:, j, :]))
                me.settle()
                dve.sem_inc(dve_passed, 1)
                for j in range(J):
                    last = v.bn_aggr(mv[n][:, j, :], stats[n][:, j, :])
                return last

            def norm(n, dst, src):
                for j in range(J):
                    last = v.tensor_scalar(dst[:, j, :], src[:, j, :], mv[n][:, j, 0:1], rstd[n][:, j:j + 1],
                                           ALU.subtract, ALU.mult)
                return last

            def ln1_stats(b, par):
                me = Own(dve, own["d0"], J, b)
                dve.wait_ge(x_in[par], 16 * (b // 2) + 16 if isinstance(b, int) else 8 * (b - par) + 16)
                ln(me, 0, xcols(b)).then_inc(ln_stats[0], 1)

            def ln1_apply(b, par):
                dve.wait_ge(ln_rstd[0], b + 1)
                wait(dve, xT_psum, b)
                norm(0, xn, xcols(b)).then_inc(xn_ready, 1)

            def time_mix(b, par):
                me = Own(dve, own["d2"], 6, b)
                dve.wait_ge(rkv_psum, b + 1)
                dve.wait_ge(exps_ready, b + 1)
                me.did(v.tensor_tensor(ekv[:, :], ps_v[par][:, :], ek[:, par, :], ALU.mult))
                me.did(v.tensor_tensor_scan(Bprev[:, 2:T], grow[:, 1:T - 1], enk[:, par, 1:T - 1], 0.0, ALU.mult, ALU.add))
                me.settle()
                me.did(v.tensor_tensor(vb[:, :], ekv[:, :], Bprev[:, :], ALU.mult))
                me.did(v.tensor_tensor_scan(Aprev[:, 2:T], decay[:, 1:T - 1], ekv[:, 1:T - 1], 0.0, ALU.mult, ALU.add))
                me.settle()
                dve.wait_ge(ekcnt_ready, b + 1)
                me.did(v.tensor_tensor(vbc[:, :], vb[:, :], ekcnt[:, par, :], ALU.add))
                me.settle()
                me.did(v.scalar_tensor_tensor(out=wkv[:, :], in0=vbc[:, :], scalar=eu[:, 0:1], in1=Aprev[:, :],
                                              op0=ALU.mult, op1=ALU.add))
                me.settle()
                me.end()
                wait(dve, attn_psum, b - 1)
                v.scalar_tensor_tensor(out=y[:, par, :], in0=th[:, par, :], scalar=1.0, in1=wkv[:, :],
                                       op0=ALU.add, op1=ALU.mult).then_inc(y_ready, 1)

            def ln2_stats(b, par):
                me = Own(dve, own["d3"], J, b)
                dve.wait_ge(attn_psum, b + 1)
                ln(me, 1, ps_attn[:, :].rearrange("p (j d) -> p j d", d=D)).then_inc(ln_stats[1], 1)

            def residual(b, par):
                me = Own(dve, own["d4"], 2 + J, b)
                dve.wait_ge(ln_rstd[1], b + 1)
                last = norm(1, an, ps_attn[:, :].rearrange("p (j d) -> p j d", d=D))
                me.did(last)
                me.settle()
                me.did(v.tensor_tensor(xcols(b), an[:, :, :], xcols(b), ALU.add))
                me.settle()
                ln(me, 2, xcols(b)).then_inc(ln_stats[2], 1)
                me.end()

            def ln3_apply(b, par):
                dve.wait_ge(ln_rstd[2], b + 1)
                if not isinstance(b, int):
                    dve.wait_ge(scattered[par], SEL * J * 8 * (b - par))
                elif b >= 2:
                    dve.wait_ge(scattered[par], SEL * J * 16 * (b // 2))
                norm(2, xf[:, par, :, :], xcols(b)).then_inc(xf_ready, 1)

            def route(b, par):
                me = Own(dve, own["d6"], 10, b)
                one, two = (chosen[:, k, :].rearrange("p (j e) -> p j e", e=E) for k in range(SEL))

                def over(small):
                    return small[:, :].rearrange("p (j a) -> p j a", a=1).to_broadcast([P, J, E])

                def do(ins):
                    me.did(ins)
                    me.settle()

                dve.wait_ge(logits_psum, b + 1)
                logits = ps_logits.rearrange("p (j e) -> p j e", e=E)
                do(v.tensor_reduce(lmax[:, :], logits, AX_X, ALU.max))
                v.tensor_tensor(ldiff[:, :, :], logits, over(lmax), ALU.subtract).then_inc(ldiff_ready, 1)
                dve.wait_ge(ldiff_ready, b + 1)
                do(v.scalar_tensor_tensor(out=cand[:, :, :], in0=ldiff[:, :, :], scalar=0.0, in1=first[:, :, :],
                                          op0=ALU.is_equal, op1=ALU.mult))
                do(v.tensor_reduce(cbest[:, :], cand[:, :, :], AX_X, ALU.max))
                do(v.tensor_tensor(one, cand[:, :, :], over(cbest), ALU.is_equal))
                do(v.scalar_tensor_tensor(out=rest[:, :, :], in0=one, scalar=LOWEST, in1=ldiff[:, :, :],
                                          op0=ALU.mult, op1=ALU.add))
                do(v.tensor_reduce(rmax[:, :], rest[:, :, :], AX_X, ALU.max))
                do(v.tensor_tensor(cand2[:, :, :], rest[:, :, :], over(rmax), ALU.is_equal))
                do(v.tensor_tensor(cand3[:, :, :], cand2[:, :, :], first[:, :, :], ALU.mult))
                do(v.tensor_reduce(cbest2[:, :], cand3[:, :, :], AX_X, ALU.max))
                do(v.tensor_tensor(two, cand3[:, :, :], over(cbest2), ALU.is_equal))
                me.end()
                v.tensor_tensor(both[:, :], chosen[:, 0, :], chosen[:, 1, :], ALU.add).then_inc(both_ready, 1)

            def place(b, par):
                me = Own(dve, own["d7"], 10, b)

                def do(ins):
                    me.did(ins)
                    me.settle()

                def twice(t):
                    return t.rearrange("p (a n) -> p a n", a=1).to_broadcast([P, SEL, J * E])

                dve.wait_ge(rank_psum, b + 1)
                do(v.tensor_tensor(rank[:, :, :], ps_rank.rearrange("p (j e) -> p j e", e=E),
                                   nextrow[:, :].rearrange("p (a e) -> p a e", a=1).to_broadcast([P, J, E]), ALU.add))
                me.did(v.tensor_tensor(nextrow[:, :], ps_total, nextrow[:, :], ALU.add))
                dve.wait_ge(expl_ready, b + 1)
                me.did(v.tensor_tensor(picked[:, :, :].rearrange("p (k j) e -> p k (j e)", k=SEL), chosen[:, :, :],
                                       twice(rank[:, :, :].rearrange("p j e -> p (j e)")), ALU.mult))
                me.did(v.tensor_tensor(pickedg[:, :, :].rearrange("p (k j) e -> p k (j e)", k=SEL), chosen[:, :, :],
                                       twice(expl[:, par, :]), ALU.mult))
                me.did(v.tensor_reduce(zsum[:, :], expl[:, par, :].rearrange("p (j e) -> p j e", e=E), AX_X, ALU.add))
                me.settle()
                me.did(v.tensor_reduce(posf[:, :], picked[:, :, :], AX_X, ALU.add))
                me.did(v.tensor_reduce(gsum[:, :, :].rearrange("p k j -> p (k j)"), pickedg[:, :, :], AX_X, ALU.add))
                me.did(v.reciprocal(zinv[:, :], zsum[:, :]))
                me.settle()
                me.did(v.tensor_copy(idx[:, par, :], posf[:, :]))
                eight = slice(b * 8, b * 8 + 8) if isinstance(b, int) else bass.ds(b * 8, 8)
                me.did(v.tensor_copy(pos_all[:, eight], posf[:, :]))
                v.scalar_tensor_tensor(out=gates_all[:, eight].rearrange("p (k j) -> p k j", k=SEL), in0=gsum[:, :, :],
                                       scalar=0.5,
                                       in1=zinv[:, :].rearrange("p (a j) -> p a j", a=1).to_broadcast([P, SEL, J]),
                                       op0=ALU.mult, op1=ALU.mult).then_inc(idx_ready, 1)
                me.end()

            def step(t, par):
                if within(t, NB):
                    ln1_stats(t, par)
                if within(t - 2, NB):
                    ln3_apply(t - 2, par)
                if within(t, NB):
                    ln1_apply(t, par)
                if within(t - 1, NB):
                    time_mix(t - 1, 1 - par)
                if within(t - 2, NB):
                    route(t - 2, par)
                if within(t - 1, NB):
                    ln2_stats(t - 1, 1 - par)
                if within(t - 2, NB):
                    place(t - 2, par)
                if within(t - 1, NB):
                    residual(t - 1, 1 - par)

            pipeline(dve, NB, 2, step)

            dc = Own(dve, own["dc"], 9, 0)

            def do(ins):
                dc.did(ins)
                dc.settle()

            dve.wait_ge(idx_ready, NB)
            dve.wait_ge(own["d7"], NB * 10)
            do(v.tensor_scalar(padrow[:, :], nextrow[:, :], lane[:, 0:1], None, ALU.add))
            v.tensor_copy(padidx[:, :], padrow[:, :]).then_inc(pads_ready, 1)
            do(v.tensor_tensor(tcount[:, :], nextrow[:, :], region0[:, :], ALU.subtract))
            do(v.tensor_tensor(tedge[:, :, :],
                               tcount[:, :].rearrange("p (e a) -> p e a", a=1).to_broadcast([P, E, TOK // P]),
                               edge0[:, :].rearrange("p (a n) -> p a n", a=1).to_broadcast([P, E, TOK // P]), ALU.is_gt))
            do(v.tensor_reduce(tnum[:, :], tedge[:, :, :], AX_X, ALU.add))
            dc.did(v.tensor_tensor_scan(tend[:, :], one8[:, :], tnum[:, :], 0.0, ALU.mult, ALU.add))
            do(v.tensor_scalar(tjump[:, :], tnum[:, :], -float(P), float(REGION), ALU.mult, ALU.add))
            slots = slotno[:, :].rearrange("p (a n) -> p a n", a=1).to_broadcast([1, E, SLOTS])
            do(v.tensor_tensor(past[:, :, :], slots,
                               tend[0:1, :].rearrange("p (e a) -> p e a", a=1).to_broadcast([1, E, SLOTS]), ALU.is_ge))
            dc.did(v.tensor_reduce(slot_e[:, :], past[:, :, :].rearrange("p e n -> p n e"), AX_X, ALU.add))
            do(v.tensor_tensor(pastj[:, :, :], past[:, :, :],
                               tjump[0:1, :].rearrange("p (e a) -> p e a", a=1).to_broadcast([1, E, SLOTS]), ALU.mult))
            dc.end()
            v.tensor_reduce(slot_r[:, :], pastj[:, :, :].rearrange("p e n -> p n e"), AX_X, ALU.add).then_inc(own["dd"], 1)
            dve.wait_ge(own["dd"], 1)
            v.tensor_scalar(slot_e[:, :], slot_e[:, :], float(E - 1), float(F), ALU.min, ALU.mult).then_inc(own["dd"], 1)
            dve.wait_ge(own["dd"], 2)
            v.tensor_copy(slot_w[:, :], slot_e[:, :]).then_inc(own["dd"], 1)
            v.scalar_tensor_tensor(out=slot_row[:, :], in0=slotno[:, :], scalar=float(P), in1=slot_r[:, :],
                                   op0=ALU.mult, op1=ALU.add).then_inc(own["dd"], 1)
            dve.wait_ge(own["dd"], 4)
            v.memset(acc[:, 0, 0:1], 0.0).then_inc(table_ready, 1)

            for e in range(E - 1):
                v.tensor_scalar(gap[:, :], pos_all[:, :], float((e + 1) * REGION), tjump[:, e:e + 1], ALU.is_ge, ALU.mult)\
                 .then_inc(own["dg"], 1)
                dve.wait_ge(own["dg"], 2 * e + 1)
                v.tensor_tensor(ypos[:, :], ypos[:, :] if e else pos_all[:, :], gap[:, :], ALU.subtract).then_inc(own["dg"], 1)
                dve.wait_ge(own["dg"], 2 * e + 2)
            v.tensor_copy(ypos_i[:, :], ypos[:, :]).then_inc(ypos_ready, 1)

            def tile(k, par):
                if within(k - 1, SLOTS):
                    dve.wait_ge(silu_ready, k)
                    dve.wait_ge(u_psum, k)
                    wait(dve, hT_psum, k - 2)
                    v.tensor_tensor(h[:, 1 - par, :], ps_u[:, :], sg[:, :], ALU.mult).then_inc(h_ready, 1)
                if within(k - 2, SLOTS):
                    dve.wait_ge(y_psum, k - 1)
                    if not isinstance(k, int):
                        dve.wait_ge(ys_out[par], 8 * (k - 2 - par))
                    elif k - 2 >= 2:
                        dve.wait_ge(ys_out[par], 16 * ((k - 2) // 2))
                    v.tensor_copy(ys[:, par, :], ps_y[:, 0:D]).then_inc(ys_ready, 1)

            pipeline(dve, SLOTS, 2, tile)

            def shared(b):
                for c in range(C):
                    dve.wait_ge(fsilu, C * b + (c + 1))
                    v.tensor_tensor(fh[:, c % 2, :], ps_fu[c % 2][:, :], fsg[:, c % 2, :], ALU.mult).then_inc(fh_ready, 1)

            def combine(b, par):
                me = Own(dve, own["c0"], 3 * J, b)
                gate = [gates_all[:, b * 8 + n:b * 8 + n + 1] if isinstance(b, int) else gates_all[:, bass.ds(b * 8 + n, 1)]
                        for n in range(SEL * J)]
                dve.wait_ge(shared_psum, b + 1)
                dve.wait_ge(gathered[par], 16 * 8 * (b // 2) + 128 if isinstance(b, int) else 64 * (b - par) + 128)
                for j in range(J):
                    me.did(v.scalar_tensor_tensor(out=acc[:, j, :], in0=gath[par][:, j, :], scalar=gate[j],
                                                  in1=ps_sh[par][:, j * P:(j + 1) * P], op0=ALU.mult, op1=ALU.add))
                me.settle()
                for j in range(J):
                    me.did(v.scalar_tensor_tensor(out=acc2[:, j, :], in0=gath[par][:, J + j, :], scalar=gate[J + j],
                                                  in1=acc[:, j, :], op0=ALU.mult, op1=ALU.add))
                me.settle()
                dve.sem_inc(dve_passed, 1)
                for j in range(J):
                    me.did(v.bn_stats(fst[:, j, :], acc2[:, j, :]))
                me.settle()
                me.end()
                dve.sem_inc(dve_passed, 1)
                v.bn_aggr(fmv[:, 0, :], fst[:, 0, :]).then_inc(shared_used, 1)
                for j in range(1, J):
                    last = v.bn_aggr(fmv[:, j, :], fst[:, j, :])
                last.then_inc(fstats, 1)
                me2 = Own(dve, own["c1"], 1, b)
                dve.wait_ge(frstd, b + 1)
                for j in range(J):
                    last = v.tensor_scalar(fn[:, j, :], acc2[:, j, :], fmv[:, j, 0:1], frs[:, j:j + 1],
                                           ALU.subtract, ALU.mult)
                me2.did(last)
                me2.settle()
                if not isinstance(b, int):
                    dve.wait_ge(out_done[par], 8 * (b - par))
                elif b >= 2:
                    dve.wait_ge(out_done[par], 16 * (b // 2))
                v.tensor_tensor(res[:, par, :, :], fn[:, :, :], xcols(b), ALU.add).then_inc(res_ready, 1)

            def both_parts(b, par):
                if within(b, NB):
                    shared(b)
                    combine(b, par)

            pipeline(dve, NB, 0, both_parts)


_INS = ['L0_attn_x', 'L0_attn_Wr', 'L0_attn_Wk', 'L0_attn_Wv', 'L0_attn_Wo', 'L0_attn_r_mu', 'L0_attn_k_mu',
        'L0_attn_v_mu', 'L0_attn_w', 'L0_attn_u', 'L0_ffn_gate_W', 'L0_ffn_w1_e', 'L0_ffn_w3_e', 'L0_ffn_w2_e',
        'L0_ffn_w1_s', 'L0_ffn_w3_s', 'L0_ffn_w2_s']
_OUTS = [((16, 512, 128), 'float32')]


def kernel(**inputs):
    import numpy as _np
    import concourse.bacc as _bacc
    from concourse import mybir as _mybir
    from concourse.bass_utils import run_bass_kernel_spmd as _run

    nc = _bacc.Bacc("TRN2", target_bir_lowering=False, num_devices=1)
    arrays, args = {}, []
    for name in _INS:
        a = _np.ascontiguousarray(inputs[name])
        arrays[f"in_{name}_dram"] = a
        args.append(nc.dram_tensor(f"in_{name}_dram", a.shape, _mybir.dt.from_np(a.dtype), kind="ExternalInput").ap())
    for i, (shape, dtype) in enumerate(_OUTS):
        dt = _mybir.dt.from_np(_np.dtype(dtype))
        args.append(nc.dram_tensor(f"out_{i}_dram", shape, dt, kind="ExternalOutput").ap())
    build(nc, *args)
    r = _run(nc, [arrays], core_ids=[0])
    return r.results[0]["out_0_dram"]
```

```python
from contextlib import ExitStack

import concourse.bass as bass
from concourse import mybir

F32 = mybir.dt.float32
F32R = mybir.dt.float32r
BF16 = mybir.dt.bfloat16
I32 = mybir.dt.int32
ALU = mybir.AluOpType
ACT = mybir.ActivationFunctionType
AX_X = mybir.AxisListType.X

P = 128
EPS = 1e-5
LOWEST = -3.0e38
CONSTS = 23


def wait(eng, sem, value):
    if isinstance(value, int) and value <= 0:
        return
    eng.wait_ge(sem, value)


class Own:

    def __init__(self, eng, sem, per, step, passed=None):
        self.eng, self.sem, self.per, self.base, self.n, self.passed = eng, sem, per, step * per, 0, passed

    def did(self, ins):
        self.n += 1
        ins.then_inc(self.sem, 1)

    def settle(self):
        self.eng.wait_ge(self.sem, self.base + self.n)
        if self.passed is not None:
            self.eng.sem_inc(self.passed, 1)

    def end(self):
        assert self.n == self.per, (self.n, self.per)


def pipeline(eng, count, skew, step):
    first, last = skew + skew % 2 + 2, count - count % 2
    for t in range(first):
        step(t, t % 2, t // 2)
    with eng.Fori(0, (last - first) // 2) as i:
        for par in range(2):
            step(2 * i + (first + par), par, i + first // 2)
    for t in range(last, count + skew):
        step(t, t % 2, t // 2)


def within(t, count):
    return not isinstance(t, int) or 0 <= t < count


def wait_turns(eng, sems, amount, n, par):
    if isinstance(n, int):
        wait(eng, sems[par], amount * (n // 2))
    else:
        eng.wait_ge(sems[par], amount // 2 * (n - par))


def build(nc, x_d, Wr_d, Wk_d, Wv_d, Wo_d, rmu_d, kmu_d, vmu_d, w_d, u_d,
          gate_d, w1_d, w3_d, w2_d, w1s_d, w3s_d, w2s_d, out_d):
    NB, T, D = x_d.shape
    E, _, F = w1_d.shape
    NS, _, FS = w1s_d.shape
    J = T // P
    C = F // P
    SEL = 2
    TOK = NB * T
    assert D == P and NS * FS == F and NB % 2 == 0 and T == F == 512
    REGION = TOK + P
    SLOTS = SEL * TOK // P + E
    ROWS = E * REGION + E * P
    XW = D + 2
    NOWHERE = float(4 * TOK)

    x_t = x_d.rearrange("b (j p) d -> b p j d", p=P)
    out_t = out_d.rearrange("b (j p) d -> b p j d", p=P)

    xs_d = nc.dram_tensor("xs_rows", [ROWS, XW], F32, kind="Internal").ap()
    ys_d = nc.dram_tensor("ys_rows", [SEL * TOK, D], F32, kind="Internal").ap()
    ys_t = ys_d.rearrange("(b j p k) d -> b p j (k d)", p=P, j=J, k=SEL)
    xfT_d = nc.dram_tensor("xfT_batches", [NB * P, T], F32, kind="Internal").ap()

    with ExitStack() as ctx:
        def sb(name, shape, dt=F32):
            return ctx.enter_context(nc.sbuf_tensor(name, shape, dt))

        def sem(name):
            return ctx.enter_context(nc.semaphore(name))

        def sem2(name):
            return [sem(name + "_even"), sem(name + "_odd")]

        bank = [ctx.enter_context(nc.psum_tensor(f"bank{n}", [P, 512], F32)) for n in range(8)]

        w13h = sb("w13h", [P, E, 2, F], F32R)
        w13l = sb("w13l", [P, E, 2, F], F32R)
        stage = sb("stage", [P, 2, F])
        w2 = sb("w2", [P, E, C, D])
        sh_h = sb("sh_h", [P, 2, F], F32R)
        sh_l = sb("sh_l", [P, 2, F], F32R)
        w2s = sb("w2s", [P, C, D])
        raw = sb("raw", [P, 4, P])
        gate_raw = sb("gate_raw", [E, P])
        mix_w = sb("mix_w", [P, 3, 2, P])
        woT = sb("woT", [P, P])
        gateT = sb("gateT", [P, E])
        mu = sb("mu", [P, 3])
        omu = sb("omu", [P, 3])
        wvec = sb("wvec", [P, 1])
        uvec = sb("uvec", [P, 1])
        eu = sb("eu", [P, 1])
        decay = sb("decay", [P, T])
        grow = sb("grow", [P, T])
        ident = sb("ident", [P, P])
        upper = sb("upper", [P, P], BF16)
        ones = sb("ones", [P, P], BF16)
        zrow = sb("zrow", [P, XW])
        first = sb("first", [P, J, E])
        cnt = sb("cnt", [P, T])
        mhalf = sb("mhalf", [P, 2 * J])

        x_all = sb("x_all", [P, NB, J * D])
        gates_all = sb("gates_all", [P, NB * 8])

        xn = sb("xn", [P, J, D])
        xT = sb("xT", [P, 2, T + 2])
        ek = sb("ek", [P, 2, T])
        enk = sb("enk", [P, 2, T])
        th = sb("th", [P, 2, T])
        ekv = sb("ekv", [P, T])
        Aprev = sb("Aprev", [P, T])
        Bprev = sb("Bprev", [P, T])
        ekcnt = sb("ekcnt", [P, 2, T])
        vb = sb("vb", [P, T])
        wfull = vb
        y = sb("y", [P, 2, T])
        an = sb("an", [P, J, D])
        xf = sb("xf", [P, 2, J, XW])
        xfT = sb("xfT", [P, 2, T])
        st = sb("st", [P, 2 * J, 6])
        st2 = sb("st2", [P, J, 6])
        mv = sb("mv", [P, 2, 2 * J, 2])
        veps, nmean = sb("veps", [P, 2, 2 * J]), sb("nmean", [P, 2, 2 * J])
        rstd, nbias = sb("rstd", [P, 2, 2 * J]), sb("nbias", [P, 2, 2 * J])
        mv2 = sb("mv2", [P, J, 2])
        veps2, nmean2 = sb("veps2", [P, J]), sb("nmean2", [P, J])
        rstd2, nbias2 = sb("rstd2", [P, J]), sb("nbias2", [P, J])

        lmax = sb("lmax", [P, J])
        ldiff = sb("ldiff", [P, J, E])
        expl = sb("expl", [P, 2, J * E])
        cand = sb("cand", [P, J, E])
        rest = sb("rest", [P, J, E])
        rmax = sb("rmax", [P, J])
        cand2 = sb("cand2", [P, J, E])
        cand3 = sb("cand3", [P, J, E])
        cbest2 = sb("cbest2", [P, J])
        chosen = sb("chosen", [P, SEL, J * E])
        both = sb("both", [P, J * E], BF16)
        nextrow = sb("nextrow", [P, E])
        rank = sb("rank", [P, J, E])
        picked = sb("picked", [P, SEL * J, E])
        posf = sb("posf", [P, SEL * J])
        idx = sb("idx", [P, 2, SEL * J], I32)
        pickedg = sb("pickedg", [P, SEL * J, E])
        gsum = sb("gsum", [P, SEL, J])
        zsum = sb("zsum", [P, J])
        zinv = sb("zinv", [P, J])

        padrow = sb("padrow", [P, E])
        padidx = sb("padidx", [P, E], I32)
        lane = sb("lane", [P, 1])
        region0 = sb("region0", [P, E])
        tcount = sb("tcount", [P, E])
        tedge = sb("tedge", [P, E, TOK // P])
        tnum = sb("tnum", [P, E])
        tend = sb("tend", [P, E])
        tjump = sb("tjump", [P, E])
        one8 = sb("one8", [P, E])
        slotno = sb("slotno", [P, SLOTS])
        edge0 = sb("edge0", [P, TOK // P])
        past = sb("past", [P, E, SLOTS])
        pastj = sb("pastj", [P, E, SLOTS])
        slot_n = sb("slot_n", [P, SLOTS])
        slot_r = sb("slot_r", [P, SLOTS])
        slot_e = sb("slot_e", [P, SLOTS])
        slot_ne = sb("slot_ne", [P, SLOTS])
        slot_ei = sb("slot_ei", [P, SLOTS], I32)
        slot_row = sb("slot_row", [P, SLOTS], I32)

        xs = sb("xs", [P, 2, XW])
        xsTh = sb("xsTh", [P, 2, P], F32R)
        xsTl = sb("xsTl", [P, 2, P], F32R)
        sg = xT[:, 0, 0:F]
        h = ek
        hT = th
        ys = sb("ys", [P, 2, D])
        row = sb("row", [P, 2])
        yrow = sb("yrow", [P, 2], I32)

        fxT = xfT
        fxTh, fxTl = w13h[:, 0, :, :], w13l[:, 0, :, :]
        fsg = ek
        fh = enk
        y2 = w2[:, 0:4, :, :].rearrange("p (q n) c d -> p q (n c d)", q=2).rearrange("p q (j n) -> p q j n", j=J)
        acc, acc2, fn = xn, ekcnt[:, :, :].rearrange("p q (j d) -> p q j d", d=D), xT[:, 0, 0:J * D].rearrange("p (j d) -> p j d", d=D)
        res = y

        consts, consts0 = sem("consts"), sem("consts0")
        w_small, w_big = sem("w_small"), sem("w_big")
        turned, setup_act, setup_dve = sem("turned"), sem("setup_act"), sem("setup_dve")
        x_in, stage_in, xfT_out, scattered = sem2("x_in"), sem2("stage_in"), sem2("xfT_out"), sem2("scattered")
        hi_ready, lo_ready = sem("hi_ready"), sem("lo_ready")
        ln13_stats, ln13_rstd = sem("ln13_stats"), sem("ln13_rstd")
        ln2_stats, ln2_rstd = sem("ln2_stats"), sem("ln2_rstd")
        xn_ready, xT_psum, xT_ready = sem("xn_ready"), sem("xT_psum"), sem("xT_ready")
        rk_psum, v_psum, exps_ready = sem("rk_psum"), sem("v_psum"), sem("exps_ready")
        ekcnt_ready, y_ready, attn_psum, an_ready = sem("ekcnt_ready"), sem("y_ready"), sem("attn_psum"), sem("an_ready")
        xf_ready, xfT_psum, xfT_ready = sem("xf_ready"), sem("xfT_psum"), sem("xfT_ready")
        logits_psum, ldiff_ready, expl_ready = sem("logits_psum"), sem("ldiff_ready"), sem("expl_ready")
        both_ready, rank_psum, idx_ready = sem("both_ready"), sem("rank_psum"), sem("idx_ready")
        pads_ready, padded, table_ready = sem("pads_ready"), sem("padded"), sem("table_ready")
        xs_in, ys_out = sem2("xs_in"), sem2("ys_out")
        xsT_psum, xsTh_ready, xsT_ready = sem("xsT_psum"), sem("xsTh_ready"), sem("xsT_ready")
        g_psum, u_psum, silu_ready, h_ready = sem("g_psum"), sem("u_psum"), sem("silu_ready"), sem("h_ready")
        hT_psum, hT_ready, y_psum, ys_ready = sem("hT_psum"), sem("hT_ready"), sem("y_psum"), sem("ys_ready")
        row_known, yrow_ready = sem("row_known"), sem("yrow_ready")
        f_in, y2_in, out_done = sem2("f_in"), sem2("y2_in"), sem2("out_done")
        fxTh_ready, fxT_ready = sem("fxTh_ready"), sem("fxT_ready")
        fgu_psum, fsilu, fh_ready = sem("fgu_psum"), sem("fsilu"), sem("fh_ready")
        down_done, shared_used = sem("down_done"), sem("shared_used")
        fstats, frstd, fn_ready, res_ready = sem("fstats"), sem("frstd"), sem("fn_ready"), sem("res_ready")
        own = {k: sem("own_" + k) for k in ("stats1", "stats3", "aggr", "mix", "ln2", "res", "route", "place", "table", "pool13", "pool2",
                                            "acc", "fln", "poolf")}
        act_passed, pool_passed, dve_passed = sem("act_passed"), sem("pool_passed"), sem("dve_passed")

        block = ctx.enter_context(nc.Block())

        ps_xT, ps_xfT, ps_r, ps_k, ps_attn, ps_small = (bank[n] for n in (0, 1, 2, 3, 6, 7))
        ps_v = (bank[4], bank[5])
        ps_logits = ps_small[:, 0:J * E]
        ps_rank = ps_small[:, J * E:2 * J * E]
        ps_total = ps_small[:, 2 * J * E:2 * J * E + E]
        ps_xsT, ps_g, ps_u, ps_hT, ps_y = (bank[n] for n in (0, 1, 2, 3, 4))
        ps_fg, ps_fu, ps_sh = bank[0:2], bank[2:4], bank[4:6]

        def xcols(b):
            v = x_all[:, b, :] if isinstance(b, int) else x_all[:, bass.ds(b, 1), :].rearrange("p a n -> p (a n)")
            return v.rearrange("p (j d) -> p j d", d=D)

        @block.sync
        def _(sp):
            for n, wd in enumerate((Wr_d, Wk_d, Wv_d, Wo_d)):
                sp.dma_start(raw[:, n, :], wd).then_inc(w_small, 16)
            for b in range(2):
                sp.dma_start(xcols(b), x_t[b]).then_inc(x_in[b], 16)
            sp.dma_start(gate_raw[:, :], gate_d).then_inc(w_small, 16)
            for n, vd in enumerate((rmu_d, kmu_d, vmu_d)):
                sp.dma_start(mu[:, n:n + 1], vd.rearrange("(d a) -> d a", a=1)).then_inc(w_small, 16)
            sp.dma_start(wvec[:, :], w_d.rearrange("(d a) -> d a", a=1)).then_inc(w_small, 16)
            sp.dma_start(uvec[:, :], u_d.rearrange("(d a) -> d a", a=1)).then_inc(w_small, 16)
            for b in range(2, NB):
                sp.wait_ge(x_in[b % 2], 16 * (b // 2))
                sp.dma_start(xcols(b), x_t[b]).then_inc(x_in[b % 2], 16)
                if b == 5:
                    sp.dma_start(w2[:, :, :, :], w2_d.rearrange("e (c f) d -> f e c d", f=P)).then_inc(w_big, 16)

            def mix(t, par, half):
                if within(t, 2 * E):
                    wait(sp, lo_ready, t - 1)
                    src = (w3_d if par else w1_d)[half if isinstance(half, int) else bass.ds(half, 1)]
                    if not isinstance(half, int):
                        src = src.rearrange("a d f -> d (a f)")
                    sp.dma_start(stage[:, par, :], src).then_inc(stage_in[par], 16)
                c = t - 4
                if within(c, NB):
                    sp.wait_ge(xfT_ready, c + 1)
                    sp.dma_start(xfT_d[c * P:(c + 1) * P, :] if isinstance(c, int) else xfT_d[bass.ds(c * P, P), :],
                                 xfT[:, par, :]).then_inc(xfT_out[par], 16)

            pipeline(sp, NB, 4, mix)

            sp.wait_ge(lo_ready, 2 * E)
            for n, wd in enumerate((w1s_d, w3s_d)):
                sp.dma_start(stage[:, n, :].rearrange("p (n f) -> p n f", f=FS), wd.rearrange("n d f -> d n f"))\
                  .then_inc(stage_in[n], 16)
            sp.dma_start(w2s[:, :, :], w2s_d.rearrange("n f d -> (n f) d").rearrange("(c f) d -> f c d", f=P)).then_inc(w_big, 16)

            sp.wait_ge(table_ready, 1)
            for q in range(2):
                sp.wait_ge(scattered[q], NB // 2 * SEL * J * 16)
            sp.wait_ge(padded, (E + 1) * 16)

            def load_slot(k, par, half):
                wait(sp, xsT_psum, k - 1)
                wait(sp, row_known, k - 1)
                row = sp.value_load(slot_row[0:1, k:k + 1] if isinstance(k, int) else slot_row[0:1, bass.ds(k, 1)],
                                    min_val=0, max_val=ROWS - P)
                sp.dma_start(xs[:, par, :], xs_d[bass.ds(row, P), :]).then_inc(xs_in[par], 16)

            pipeline(sp, SLOTS, 0, load_slot)

            for q in range(2):
                sp.wait_ge(xfT_out[q], NB // 2 * 16)

            def carry(n, par, half):
                if within(n, NB):
                    wait(sp, fxT_ready, n - 1)
                    sp.dma_start(fxT[:, par, :], xfT_d[n * P:(n + 1) * P, :] if isinstance(n, int)
                                 else xfT_d[bass.ds(n * P, P), :]).then_inc(f_in[par], 16)
                if isinstance(n, int) and n == 1:
                    for q in range(2):
                        sp.wait_ge(ys_out[q], SLOTS // 2 * 16)
                b = n - 1
                if within(b, NB):
                    wait(sp, shared_used, b - 1)
                    src = ys_t[b] if isinstance(b, int) else ys_t[bass.ds(b, 1)].rearrange("a p j d -> p (a j) d")
                    sp.dma_start(y2[:, 1 - par, :, :], src).then_inc(y2_in[1 - par], 16)
                o = n - 4
                if within(o, NB):
                    sp.wait_ge(res_ready, o + 1)
                    dst = out_t[o] if isinstance(o, int) else out_t[bass.ds(o, 1)].rearrange("a p j d -> p (a j) d")
                    sp.dma_start(dst, res[:, par, :].rearrange("p (j d) -> p j d", d=D)).then_inc(out_done[par], 16)

            pipeline(sp, NB, 4, carry)
            for q in range(2):
                sp.wait_ge(out_done[q], NB // 2 * 16)

        @block.gpsimd
        def _(pool):
            g = nc.gpsimd
            g.memset(ident[:, :], 0.0).then_inc(consts0, 1)
            g.memset(upper[:, :], 0.0).then_inc(consts0, 1)
            n = 0

            def const(ins):
                nonlocal n
                n += 1
                ins.then_inc(consts, 1)

            def numbers(out, pattern, base=0, per_partition=0):
                const(g.iota(out, pattern=pattern, base=base, channel_multiplier=per_partition,
                             allow_small_or_imprecise_dtypes=True))

            for tile, value in ((ones[:, :], 1.0), (zrow[:, 0:D], 0.0), (zrow[:, D:D + 1], NOWHERE),
                                (zrow[:, D + 1:XW], 0.0), (mhalf[:, :], -0.5), (one8[:, :], 1.0),
                                (xT[:, 0, 0:2], 0.0), (xT[:, 1, 0:2], 0.0), (Aprev[:, 0:2], 0.0), (Bprev[:, 0:2], 0.0),
                                (cnt[:, 0:1], 0.0), (mv[:, :, :, :], 1.0)):
                const(g.memset(tile, value))
            numbers(first[:, :, :], [[0, J], [-1, E]], base=E)
            numbers(cnt[:, 1:T], [[1, T - 1]])
            numbers(nextrow[:, :], [[REGION, E]])
            numbers(region0[:, :], [[REGION, E]])
            numbers(lane[:, :], [[0, 1]], per_partition=1)
            numbers(slotno[:, :], [[1, SLOTS]])
            numbers(edge0[:, :], [[P, TOK // P]])
            for q in range(2):
                numbers(xf[:, q, :, D], [[2 * P, J]], base=2 * T * (q - 2), per_partition=2)
            pool.wait_ge(consts0, 2)
            const(g.affine_select(out=ident[:, :], in_=ident[:, :], compare_op=ALU.not_equal, fill=1.0, base=0,
                                  pattern=[[-1, P]], channel_multiplier=1))
            const(g.affine_select(out=upper[:, :], in_=upper[:, :], compare_op=ALU.is_ge, fill=1.0, base=0,
                                  pattern=[[-1, P]], channel_multiplier=1))
            assert n == CONSTS
            pool.wait_ge(consts, CONSTS)

            def rsqrt(me, stats_sem, count, ve, nm, rs, nb, done, width):
                pool.wait_ge(stats_sem, count)
                pool.sem_inc(pool_passed, 1)
                me.did(g.tensor_tensor(rs, ve, mhalf[:, 0:width], ALU.pow))
                me.settle()
                g.tensor_tensor(nb, nm, rs, ALU.mult).then_inc(done, 1)
                me.end()

            def step(t, par, half):
                m, b, c, d = t - 2, t - 3, t - 4, t - 5

                def scatter(k, js, q):
                    for j in js:
                        pool.indirect_dma_start(
                            xs_d[:, :], bass.IndirectOffsetOnAxis(ap=idx[:, q, k * J + j:k * J + j + 1], axis=0),
                            xf[:, q, j, :], None).then_inc(scattered[q], 16)

                if within(b, NB):
                    rsqrt(Own(pool, own["pool2"], 1, b, pool_passed), ln2_stats, b + 1,
                          veps2[:, :], nmean2[:, :], rstd2[:, :], nbias2[:, :], ln2_rstd, J)
                if within(m, NB):
                    pool.wait_ge(exps_ready, m + 1)
                    pool.sem_inc(pool_passed, 1)
                    wait(pool, y_ready, m - 1)
                    pool.sem_inc(pool_passed, 1)
                    g.tensor_tensor(ekcnt[:, par, :], ek[:, par, :], cnt[:, :], ALU.mult).then_inc(ekcnt_ready, 1)
                if within(d, NB):
                    scatter(1, range(1, J), 1 - par)
                if within(t, NB + 3):
                    rsqrt(Own(pool, own["pool13"], 1, t, pool_passed), ln13_stats, t + 1,
                          veps[:, par, :], nmean[:, par, :], rstd[:, par, :], nbias[:, par, :], ln13_rstd, 2 * J)
                if within(c, NB):
                    pool.wait_ge(idx_ready, c + 1)
                    pool.sem_inc(pool_passed, 1)
                    scatter(0, range(J), par)
                    scatter(1, range(1), par)

            pipeline(pool, NB, 5, step)

            pool.wait_ge(pads_ready, 1)
            for e in range(E):
                pool.indirect_dma_start(xs_d[:, :], bass.IndirectOffsetOnAxis(ap=padidx[:, e:e + 1], axis=0),
                                        zrow[:, :], None).then_inc(padded, 16)
            pool.dma_start(xs_d[E * REGION:ROWS, :].rearrange("(a p) d -> p a d", p=P),
                           zrow[:, :].rearrange("p (a d) -> p a d", a=1).to_broadcast([P, E, XW])).then_inc(padded, 16)

            def spread(k, par, half):
                pool.wait_ge(ys_ready, k + 1)
                pool.sem_inc(pool_passed, 1)
                pool.indirect_dma_start(ys_d[:, :], bass.IndirectOffsetOnAxis(ap=yrow[:, par:par + 1], axis=0),
                                        ys[:, par, :], None, bounds_check=SEL * TOK - 1, oob_is_err=False)\
                    .then_inc(ys_out[par], 16)

            pipeline(pool, SLOTS, 0, spread)

            def last_norm(b, par, half):
                if within(b, NB):
                    rsqrt(Own(pool, own["poolf"], 1, b, pool_passed), fstats, b + 1,
                          veps2[:, :], nmean2[:, :], rstd2[:, :], nbias2[:, :], frstd, J)

            pipeline(pool, NB, 0, last_norm)

        @block.scalar
        def _(act):
            s = nc.scalar
            act.wait_ge(w_small, 160)
            s.activation(eu[:, :], uvec[:, :], ACT.Exp).then_inc(setup_act, 1)
            act.wait_ge(setup_dve, 2)
            s.activation(decay[:, :], wfull[:, :], ACT.Exp, scale=-1.0).then_inc(setup_act, 1)
            s.activation(grow[:, :], wfull[:, :], ACT.Exp).then_inc(setup_act, 1)
            act.wait_ge(consts, CONSTS)

            def norm(dst, src, rs, nb):
                for j in range(J):
                    last = s.activation(dst(j), src[:, j, :], ACT.Identity, bias=nb[:, j:j + 1], scale=rs[:, j:j + 1])
                return last

            def step(t, par, half):
                m, b, c = t - 2, t - 3, t - 4
                if within(m, NB):
                    act.wait_ge(ln13_rstd, m + 1)
                    wait(act, xT_psum, m)
                    act.sem_inc(act_passed, 1)
                    norm(lambda j: xn[:, j, :], xcols(m), rstd[:, par, 0:J], nbias[:, par, 0:J]).then_inc(xn_ready, 1)
                if within(t, 2 * E):
                    act.wait_ge(stage_in[par], 16 * half + 16)
                    act.sem_inc(act_passed, 1)
                    s.activation(w13h[:, half, par, :] if isinstance(half, int)
                                 else w13h[:, bass.ds(half, 1), par, :].rearrange("p a f -> p (a f)"),
                                 stage[:, par, :], ACT.Copy).then_inc(hi_ready, 1)
                if within(m, NB):
                    act.wait_ge(xT_psum, m + 1)
                    wait(act, v_psum, m - 1)
                    s.activation(xT[:, par, 2:T + 2], ps_xT[:, :], ACT.Copy).then_inc(xT_ready, 1)
                if within(c, NB):
                    act.wait_ge(ln13_rstd, t)
                    wait_turns(act, scattered, SEL * J * 16, c, par)
                    act.sem_inc(act_passed, 1)
                    norm(lambda j: xf[:, par, j, 0:D], xcols(c), rstd[:, 1 - par, J:2 * J], nbias[:, 1 - par, J:2 * J])\
                        .then_inc(xf_ready, 1)
                    act.wait_ge(xfT_psum, c + 1)
                    wait(act, logits_psum, c - 1)
                    wait_turns(act, xfT_out, 16, c, par)
                    s.activation(xfT[:, par, :], ps_xfT[:, :], ACT.Copy).then_inc(xfT_ready, 1)
                if within(m, NB):
                    act.wait_ge(rk_psum, m + 1)
                    wait(act, y_ready, m - 1)
                    wait(act, ekcnt_ready, m - 1)
                    s.activation(th[:, par, :], ps_r[:, :], ACT.Tanh, scale=0.5)
                    s.activation(enk[:, par, :], ps_k[:, :], ACT.Exp, scale=-1.0)
                    s.activation(ek[:, par, :], ps_k[:, :], ACT.Exp).then_inc(exps_ready, 1)
                if within(c, NB):
                    act.wait_ge(ldiff_ready, c + 1)
                    s.activation(expl[:, par, :], ldiff[:, :, :].rearrange("p j e -> p (j e)"), ACT.Exp)\
                     .then_inc(expl_ready, 1)
                if within(b, NB):
                    act.wait_ge(ln2_rstd, b + 1)
                    norm(lambda j: an[:, j, :], ps_attn[:, :].rearrange("p (j d) -> p j d", d=D), rstd2, nbias2)\
                        .then_inc(an_ready, 1)

            pipeline(act, NB, 4, step)

            for n in range(2):
                act.wait_ge(stage_in[n], 16 * E + 16)
                s.activation(sh_h[:, n, :], stage[:, n, :], ACT.Copy).then_inc(hi_ready, 1)

            act.wait_ge(y_ready, NB)
            act.wait_ge(v_psum, NB)

            def tile(k, par, half):
                if within(k - 3, SLOTS):
                    q = 1 - par
                    act.wait_ge(y_psum, k - 2)
                    act.wait_ge(yrow_ready, k - 2)
                    if not isinstance(k, int):
                        act.wait_ge(ys_out[q], 8 * (k - 3 - (1 - par)))
                    elif k - 3 >= 2:
                        act.wait_ge(ys_out[q], 16 * ((k - 3) // 2))
                    s.activation(ys[:, q, :], ps_y[:, 0:D], ACT.Copy).then_inc(ys_ready, 1)
                if within(k, SLOTS):
                    act.wait_ge(xsT_psum, k + 1)
                    wait(act, u_psum, k - 1)
                    s.activation(xsTh[:, par, :], ps_xsT[:, 0:P], ACT.Copy).then_inc(xsTh_ready, 1)
                if within(k - 2, SLOTS):
                    act.wait_ge(hT_psum, k - 1)
                    wait(act, y_psum, k - 3)
                    s.activation(hT[:, par, :], ps_hT[:, :], ACT.Copy).then_inc(hT_ready, 1)
                if within(k - 1, SLOTS):
                    act.wait_ge(g_psum, k)
                    wait(act, h_ready, k - 1)
                    s.activation(sg, ps_g[:, :], ACT.Silu).then_inc(silu_ready, 1)

            pipeline(act, SLOTS, 3, tile)

            act.wait_ge(h_ready, SLOTS)
            act.wait_ge(hT_psum, SLOTS)

            def shared(t, par, half):
                m, r = t - 1, t - 3

                def silu(c):
                    if within(m, NB):
                        act.wait_ge(fgu_psum, C * m + (c + 1))
                        wait(act, fh_ready, C * m + (c - 1))
                        s.activation(fsg[:, c % 2, :], ps_fg[c % 2][:, :], ACT.Silu).then_inc(fsilu, 1)

                def part(js):
                    if within(r, NB):
                        for j in js:
                            last = s.activation(fn[:, j, :], acc2[:, 1 - par, j, :], ACT.Identity,
                                                bias=nbias2[:, j:j + 1], scale=rstd2[:, j:j + 1])
                        return last

                silu(0)
                if within(r, NB):
                    act.wait_ge(frstd, r + 1)
                    wait(act, res_ready, r)
                part(range(0, J // 2))
                silu(1)
                last = part(range(J // 2, J))
                if within(r, NB):
                    last.then_inc(fn_ready, 1)
                silu(2)
                if within(t, NB):
                    act.wait_ge(f_in[par], 16 * half + 16)
                    wait(act, fgu_psum, C * (t - 1))
                    s.activation(fxTh[:, par, :], fxT[:, par, :], ACT.Copy).then_inc(fxTh_ready, 1)
                silu(3)

            pipeline(act, NB, 3, shared)

        @block.tensor
        def _(pe):
            p = nc.tensor
            pe.wait_ge(w_small, 160)
            pe.wait_ge(consts, CONSTS)
            for n in range(4):
                p.transpose(bank[0][:, n * P:(n + 1) * P], raw[:, n, :], ident[:, :])
            p.transpose(bank[1][:, 0:E], gate_raw[:, :], ident[0:E, 0:E]).then_inc(turned, 1)
            pe.wait_ge(setup_dve, 11)

            def step(t, par, half):
                m, b, c = t - 2, t - 3, t - 4

                def project(n, dst):
                    p.matmul(dst[:, :], mix_w[:, n, 0, :], xT[:, par, 2:T + 2], start=True, stop=False)
                    return p.matmul(dst[:, :], mix_w[:, n, 1, :], xT[:, par, 1:T + 1], start=False, stop=True)

                if within(m, NB):
                    pe.wait_ge(xn_ready, m + 1)
                    wait(pe, xT_ready, m)
                    for j in range(J):
                        last = p.transpose(ps_xT[:, j * P:(j + 1) * P], xn[:, j, :], ident[:, :])
                    last.then_inc(xT_psum, 1)
                    pe.wait_ge(xT_ready, m + 1)
                    wait(pe, exps_ready, m)
                    project(0, ps_r)
                    project(1, ps_k).then_inc(rk_psum, 1)
                if within(c, NB):
                    pe.wait_ge(xf_ready, c + 1)
                    wait(pe, xfT_ready, c)
                    for j in range(J):
                        last = p.transpose(ps_xfT[:, j * P:(j + 1) * P], xf[:, par, j, 0:D], ident[:, :])
                    last.then_inc(xfT_psum, 1)
                if within(b, NB):
                    pe.wait_ge(y_ready, b + 1)
                    wait(pe, an_ready, b)
                    for j in range(J):
                        last = p.matmul(ps_attn[:, j * P:(j + 1) * P], y[:, 1 - par, j * P:(j + 1) * P], woT[:, :],
                                        start=True, stop=True)
                    last.then_inc(attn_psum, 1)
                if within(c, NB):
                    pe.wait_ge(xfT_ready, c + 1)
                    wait(pe, idx_ready, c)
                    for j in range(J):
                        last = p.matmul(ps_logits[:, j * E:(j + 1) * E], xfT[:, par, j * P:(j + 1) * P], gateT[:, :],
                                        start=True, stop=True)
                    last.then_inc(logits_psum, 1)
                if within(m, NB):
                    wait(pe, y_ready, m - 1)
                    project(2, ps_v[par]).then_inc(v_psum, 1)
                if within(c, NB):
                    pe.wait_ge(both_ready, c + 1)
                    p.matmul(ps_rank, upper[:, :], both[:, :], start=True, stop=False)
                    for j in range(1, J):
                        p.matmul(ps_rank[:, j * E:J * E], ones[:, :], both[:, 0:(J - j) * E], start=False, stop=(j == J - 1))
                    for j in range(J):
                        last = p.matmul(ps_total, ones[:, :], both[:, j * E:(j + 1) * E], start=(j == 0), stop=(j == J - 1))
                    last.then_inc(rank_psum, 1)

            pipeline(pe, NB, 4, step)

            def split(dst, left, right, last_stop=True):
                (lh, ll), (rh, rl) = left, right
                p.matmul(dst, ll, rh, start=True, stop=False)
                p.matmul(dst, lh, rl, start=False, stop=False)
                return p.matmul(dst, lh, rh, start=False, stop=True)

            pe.wait_ge(w_big, 32)
            pe.wait_ge(lo_ready, 2 * E)
            pe.wait_ge(table_ready, 1)

            def expert(k):
                return pe.value_load(slot_ei[0:1, k:k + 1] if isinstance(k, int) else slot_ei[0:1, bass.ds(k, 1)],
                                     min_val=0, max_val=E - 1)

            known = [None]

            def tile(k, par, half):
                def up(dst, e, n):
                    wh, wl = (w[:, bass.ds(e, 1), n, :].rearrange("p a f -> p (a f)") for w in (w13h, w13l))
                    return split(dst[:, :], (xsTh[:, 1 - par, :], xsTl[:, 1 - par, :]), (wh, wl))

                e = expert(k - 1) if within(k - 1, SLOTS) else None
                if within(k - 2, SLOTS):
                    pe.wait_ge(h_ready, k - 1)
                    for c in range(C):
                        last = p.transpose(ps_hT[:, c * P:(c + 1) * P], h[:, par, c * P:(c + 1) * P], ident[:, :])
                    last.then_inc(hT_psum, 1)
                elif within(k - 1, SLOTS):
                    pe.wait_ge(xsT_ready, k)
                if within(k, SLOTS):
                    pe.wait_ge(xs_in[par], 16 * half + 16)
                    p.transpose(ps_xsT[:, 0:P], xs[:, par, 0:D], ident[:, :]).then_inc(xsT_psum, 1)
                if within(k - 1, SLOTS):
                    up(ps_g, e, 0).then_inc(g_psum, 1)
                    up(ps_u, e, 1).then_inc(u_psum, 1)
                if within(k - 2, SLOTS):
                    e2 = known[0] if par else expert(k - 2)
                    pe.wait_ge(hT_ready, k - 1)
                    for c in range(C):
                        last = p.matmul(ps_y[:, 0:D], hT[:, par, c * P:(c + 1) * P],
                                        w2[:, bass.ds(e2, 1), c, :].rearrange("p a d -> p (a d)"),
                                        start=(c == 0), stop=(c == C - 1))
                    last.then_inc(y_psum, 1)
                known[0] = e

            pipeline(pe, SLOTS, 2, tile)

            pe.wait_ge(lo_ready, 2 * E + 2)
            pe.wait_ge(ys_ready, SLOTS)

            def shared(m, par, half):
                def up(c):
                    wait(pe, fh_ready, C * m + (c - 1))
                    x = (fxTh[:, par, :], fxTl[:, par, :])
                    for n, dst in enumerate((ps_fg, ps_fu)):
                        last = split(dst[c % 2][:, :], (sh_h[:, n, c * P:(c + 1) * P], sh_l[:, n, c * P:(c + 1) * P]), x)
                    last.then_inc(fgu_psum, 1)

                def down(b, q, c):
                    pe.wait_ge(fh_ready, C * b + (c + 1))
                    if c == 0:
                        wait(pe, shared_used, b - 1)
                    for j in range(J):
                        last = p.matmul(ps_sh[q][:, j * P:(j + 1) * P], fh[:, c % 2, j * P:(j + 1) * P], w2s[:, c, :],
                                        start=(c == 0 and j == 0), stop=(c == C - 1), skip_group_check=True)
                    last.then_inc(down_done, 1)

                if within(m, NB):
                    pe.wait_ge(fxT_ready, m + 1)
                    up(0)
                if within(m - 1, NB):
                    down(m - 1, 1 - par, C - 1)
                if within(m, NB):
                    for c in range(1, C):
                        up(c)
                        down(m, par, c - 1)

            pipeline(pe, NB, 1, shared)

        @block.vector
        def _(dve):
            v = nc.vector
            dve.wait_ge(w_small, 160)
            dve.wait_ge(consts, CONSTS)
            v.memset(wfull[:, :], 0.0).then_inc(setup_dve, 1)
            dve.wait_ge(setup_dve, 1)
            v.tensor_scalar(wfull[:, :], wfull[:, :], wvec[:, 0:1], None, ALU.add).then_inc(setup_dve, 1)
            v.tensor_scalar(omu[:, :], mu[:, :], -1.0, 1.0, ALU.mult, ALU.add).then_inc(setup_dve, 1)
            dve.wait_ge(setup_dve, 3)
            dve.wait_ge(turned, 1)
            for n in range(3):
                src = bank[0][:, n * P:(n + 1) * P]
                v.tensor_scalar(mix_w[:, n, 0, :], src, mu[:, n:n + 1], None, ALU.mult).then_inc(setup_dve, 1)
                v.tensor_scalar(mix_w[:, n, 1, :], src, omu[:, n:n + 1], None, ALU.mult).then_inc(setup_dve, 1)
            v.tensor_scalar(woT[:, :], bank[0][:, 3 * P:4 * P], 0.5, None, ALU.mult).then_inc(setup_dve, 1)
            v.tensor_copy(gateT[:, :], bank[1][:, 0:E]).then_inc(setup_dve, 1)
            dve.wait_ge(setup_act, 3)

            def over(small):
                return small.rearrange("p (j a) -> p j a", a=1).to_broadcast([P, J, E])

            def step(t, par, half):
                b, c, bp, cp = t - 3, t - 4, 1 - par, par
                has_a, has_b, has_c = within(t, NB), within(b, NB), within(c, NB)
                stats1 = Own(dve, own["stats1"], J, t)
                stats3 = Own(dve, own["stats3"], J, b)
                aggr = Own(dve, own["aggr"], 1, t)
                mix = Own(dve, own["mix"], 6, b)
                ln2 = Own(dve, own["ln2"], J + 1, b)
                rsd = Own(dve, own["res"], 1, b)
                route = Own(dve, own["route"], 10, c)
                place = Own(dve, own["place"], 10, c)
                one, two = (chosen[:, k, :].rearrange("p (j e) -> p j e", e=E) for k in range(SEL))
                logits = ps_logits.rearrange("p (j e) -> p j e", e=E)
                best = xf[:, cp, :, D + 1]

                def low():
                    dve.wait_ge(hi_ready, t + 1)
                    if isinstance(half, int):
                        hi, lo = w13h[:, half, par, :], w13l[:, half, par, :]
                    else:
                        hi, lo = (w[:, bass.ds(half, 1), par, :].rearrange("p a f -> p (a f)") for w in (w13h, w13l))
                    v.tensor_tensor(lo, stage[:, par, :], hi.bitcast(F32), ALU.subtract).then_inc(lo_ready, 1)

                def m_ekv():
                    dve.wait_ge(v_psum, b + 1)
                    dve.wait_ge(exps_ready, b + 1)
                    mix.did(v.tensor_tensor(ekv[:, :], ps_v[bp][:, :], ek[:, bp, :], ALU.mult))

                def m_bprev():
                    mix.did(v.tensor_tensor_scan(Bprev[:, 2:T], grow[:, 1:T - 1], enk[:, bp, 1:T - 1], 0.0,
                                                 ALU.mult, ALU.add))

                def m_vb():
                    mix.settle()
                    mix.did(v.tensor_tensor(vb[:, :], ekv[:, :], Bprev[:, :], ALU.mult))

                def m_aprev():
                    mix.did(v.tensor_tensor_scan(Aprev[:, 2:T], decay[:, 1:T - 1], ekv[:, 1:T - 1], 0.0,
                                                 ALU.mult, ALU.add))

                def m_cnt():
                    mix.settle()
                    dve.wait_ge(ekcnt_ready, b + 1)
                    mix.did(v.tensor_tensor(vb[:, :], vb[:, :], ekcnt[:, bp, :], ALU.add))

                def m_wkv():
                    mix.settle()
                    mix.did(v.scalar_tensor_tensor(out=vb[:, :], in0=vb[:, :], scalar=eu[:, 0:1], in1=Aprev[:, :],
                                                   op0=ALU.mult, op1=ALU.add))

                def m_y():
                    mix.settle()
                    mix.end()
                    wait(dve, attn_psum, b - 1)
                    v.scalar_tensor_tensor(out=y[:, bp, :], in0=th[:, bp, :], scalar=1.0, in1=vb[:, :],
                                           op0=ALU.add, op1=ALU.mult).then_inc(y_ready, 1)

                def l_stats(j):
                    if j == 0:
                        dve.wait_ge(attn_psum, b + 1)
                        dve.sem_inc(dve_passed, 1)
                    ln2.did(v.bn_stats(st2[:, j, :], ps_attn[:, j * P:(j + 1) * P]))

                def l_aggr():
                    ln2.settle()
                    dve.sem_inc(dve_passed, 1)
                    for j in range(J):
                        last = v.bn_aggr(mv2[:, j, :], st2[:, j, :])
                    ln2.did(last)

                def l_done():
                    ln2.settle()
                    ln2.end()
                    wait(dve, an_ready, b)
                    v.tensor_scalar(veps2[:, :], mv2[:, :, 1], EPS, None, ALU.add)
                    v.tensor_scalar(nmean2[:, :], mv2[:, :, 0], -1.0, None, ALU.mult).then_inc(ln2_stats, 1)

                def r_max():
                    dve.wait_ge(logits_psum, c + 1)
                    route.did(v.tensor_reduce(lmax[:, :], logits, AX_X, ALU.max))

                def r_diff():
                    route.settle()
                    wait(dve, expl_ready, c)
                    v.tensor_tensor(ldiff[:, :, :], logits, over(lmax[:, :]), ALU.subtract).then_inc(ldiff_ready, 1)

                def r_cand():
                    dve.wait_ge(ldiff_ready, c + 1)
                    route.did(v.scalar_tensor_tensor(out=cand[:, :, :], in0=ldiff[:, :, :], scalar=0.0,
                                                     in1=first[:, :, :], op0=ALU.is_equal, op1=ALU.mult))

                def r_best():
                    route.settle()
                    wait_turns(dve, scattered, SEL * J * 16, c, cp)
                    route.did(v.tensor_reduce(best, cand[:, :, :], AX_X, ALU.max))

                def r_one():
                    route.settle()
                    route.did(v.tensor_tensor(one, cand[:, :, :], over(best), ALU.is_equal))

                def r_rest():
                    route.settle()
                    route.did(v.scalar_tensor_tensor(out=rest[:, :, :], in0=one, scalar=LOWEST, in1=ldiff[:, :, :],
                                                     op0=ALU.mult, op1=ALU.add))

                def r_rmax():
                    route.settle()
                    route.did(v.tensor_reduce(rmax[:, :], rest[:, :, :], AX_X, ALU.max))

                def r_cand2():
                    route.settle()
                    route.did(v.tensor_tensor(cand2[:, :, :], rest[:, :, :], over(rmax[:, :]), ALU.is_equal))

                def r_cand3():
                    route.settle()
                    route.did(v.tensor_tensor(cand3[:, :, :], cand2[:, :, :], first[:, :, :], ALU.mult))

                def r_best2():
                    route.settle()
                    route.did(v.tensor_reduce(cbest2[:, :], cand3[:, :, :], AX_X, ALU.max))

                def r_two():
                    route.settle()
                    route.did(v.tensor_tensor(two, cand3[:, :, :], over(cbest2[:, :]), ALU.is_equal))

                def r_both():
                    route.settle()
                    route.end()
                    v.tensor_tensor(both[:, :], chosen[:, 0, :], chosen[:, 1, :], ALU.add).then_inc(both_ready, 1)

                def twice(x):
                    return x.rearrange("p (a n) -> p a n", a=1).to_broadcast([P, SEL, J * E])

                def p_gates():
                    dve.wait_ge(expl_ready, c + 1)
                    place.did(v.tensor_tensor(pickedg[:, :, :].rearrange("p (k j) e -> p k (j e)", k=SEL), chosen[:, :, :],
                                              twice(expl[:, cp, :]), ALU.mult))
                    place.did(v.tensor_reduce(zsum[:, :], expl[:, cp, :].rearrange("p (j e) -> p j e", e=E), AX_X, ALU.add))
                    place.did(v.tensor_scalar(xf[:, cp, :, D], xf[:, cp, :, D], float(2 * 2 * T), None, ALU.add))
                    place.settle()
                    place.did(v.tensor_reduce(gsum[:, :, :].rearrange("p k j -> p (k j)"), pickedg[:, :, :], AX_X, ALU.add))
                    place.did(v.reciprocal(zinv[:, :], zsum[:, :]))

                def p_rank():
                    dve.wait_ge(rank_psum, c + 1)
                    place.did(v.tensor_tensor(rank[:, :, :], ps_rank.rearrange("p (j e) -> p j e", e=E),
                                              nextrow[:, :].rearrange("p (a e) -> p a e", a=1).to_broadcast([P, J, E]),
                                              ALU.add))

                def p_gates2():
                    place.settle()
                    place.did(v.tensor_tensor(nextrow[:, :], ps_total, nextrow[:, :], ALU.add))
                    eight = slice(c * 8, c * 8 + 8) if isinstance(c, int) else bass.ds(c * 8, 8)
                    place.did(v.scalar_tensor_tensor(
                        out=gates_all[:, eight].rearrange("p (k j) -> p k j", k=SEL), in0=gsum[:, :, :], scalar=0.5,
                        in1=zinv[:, :].rearrange("p (a j) -> p a j", a=1).to_broadcast([P, SEL, J]),
                        op0=ALU.mult, op1=ALU.mult))

                def p_pick():
                    place.did(v.tensor_tensor(picked[:, :, :].rearrange("p (k j) e -> p k (j e)", k=SEL), chosen[:, :, :],
                                              twice(rank[:, :, :].rearrange("p j e -> p (j e)")), ALU.mult))

                def p_rows():
                    place.settle()
                    place.did(v.tensor_reduce(posf[:, :], picked[:, :, :], AX_X, ALU.add))
                    place.settle()
                    place.end()
                    v.tensor_copy(idx[:, cp, :], posf[:, :]).then_inc(idx_ready, 1)

                def residual():
                    dve.wait_ge(an_ready, b + 1)
                    rsd.did(v.tensor_tensor(xcols(b), an[:, :, :], xcols(b), ALU.add))

                def stats_of_b(j):
                    if j == 0:
                        rsd.settle()
                        rsd.end()
                        dve.sem_inc(dve_passed, 1)
                    stats3.did(v.bn_stats(st[:, J + j, :], xcols(b)[:, j, :]))

                def run(has, *parts):
                    if has:
                        for part in parts:
                            part() if callable(part) else part[0](*part[1:])

                run(has_b, m_ekv, m_bprev, m_vb, m_aprev, m_cnt, m_wkv, m_y)
                if within(t, 2 * E):
                    low()
                if has_a:
                    dve.wait_ge(x_in[par], 16 * half + 16)
                    dve.sem_inc(dve_passed, 1)
                    for j in range(J):
                        stats1.did(v.bn_stats(st[:, j, :], xcols(t)[:, j, :]))
                for j in range(J):
                    run(has_b, (l_stats, j))
                run(has_b, l_aggr)
                run(has_c, r_max, r_diff)
                run(has_b, l_done)
                run(has_c, r_cand, r_best, r_one, r_rest, r_rmax, r_cand2, r_cand3, r_best2, r_two, r_both, p_gates)
                run(has_b, residual)
                for j in range(J):
                    run(has_b, (stats_of_b, j))
                if has_a or has_b:
                    if has_a:
                        stats1.settle()
                    if has_b:
                        stats3.settle()
                    dve.sem_inc(dve_passed, 1)
                    wait(dve, xn_ready, min(t - 1, NB) if isinstance(t, int) else t - 1)
                    wait(dve, xf_ready, t - 4)
                    dve.sem_inc(dve_passed, 1)
                    for j in range(2 * J):
                        if (j < J and has_a) or (j >= J and has_b):
                            last = v.bn_aggr(mv[:, par, j, :], st[:, j, :])
                    aggr.did(last)
                    aggr.settle()
                    v.tensor_scalar(veps[:, par, :], mv[:, par, :, 1], EPS, None, ALU.add)
                    v.tensor_scalar(nmean[:, par, :], mv[:, par, :, 0], -1.0, None, ALU.mult).then_inc(ln13_stats, 1)
                run(has_c, p_rank, p_gates2, p_pick, p_rows)

            pipeline(dve, NB, 4, step)

            dc = Own(dve, own["table"], 13, 0)

            def do(ins):
                dc.did(ins)
                dc.settle()

            for n in range(2):
                dve.wait_ge(hi_ready, 2 * E + n + 1)
                v.tensor_tensor(sh_l[:, n, :], stage[:, n, :], sh_h[:, n, :].bitcast(F32), ALU.subtract).then_inc(lo_ready, 1)
            dve.wait_ge(w_big, 32)
            do(v.tensor_scalar(w2s[:, :, :], w2s[:, :, :], 0.5 / NS, None, ALU.mult))
            dve.wait_ge(own["place"], NB * 10)
            do(v.tensor_scalar(padrow[:, :], nextrow[:, :], lane[:, 0:1], None, ALU.add))
            v.tensor_copy(padidx[:, :], padrow[:, :]).then_inc(pads_ready, 1)
            do(v.tensor_tensor(tcount[:, :], nextrow[:, :], region0[:, :], ALU.subtract))
            do(v.tensor_tensor(tedge[:, :, :],
                               tcount[:, :].rearrange("p (e a) -> p e a", a=1).to_broadcast([P, E, TOK // P]),
                               edge0[:, :].rearrange("p (a n) -> p a n", a=1).to_broadcast([P, E, TOK // P]), ALU.is_gt))
            do(v.tensor_reduce(tnum[:, :], tedge[:, :, :], AX_X, ALU.add))
            dc.did(v.tensor_tensor_scan(tend[:, :], one8[:, :], tnum[:, :], 0.0, ALU.mult, ALU.add))
            do(v.tensor_scalar(tjump[:, :], tnum[:, :], -float(P), float(REGION), ALU.mult, ALU.add))
            slots = slotno[:, :].rearrange("p (a n) -> p a n", a=1).to_broadcast([P, E, SLOTS])
            do(v.tensor_tensor(past[:, :, :], slots,
                               tend[:, :].rearrange("p (e a) -> p e a", a=1).to_broadcast([P, E, SLOTS]), ALU.is_ge))
            dc.did(v.tensor_reduce(slot_n[:, :], past[:, :, :].rearrange("p e n -> p n e"), AX_X, ALU.add))
            do(v.tensor_tensor(pastj[:, :, :], past[:, :, :],
                               tjump[:, :].rearrange("p (e a) -> p e a", a=1).to_broadcast([P, E, SLOTS]), ALU.mult))
            dc.did(v.tensor_reduce(slot_r[:, :], pastj[:, :, :].rearrange("p e n -> p n e"), AX_X, ALU.add))
            do(v.tensor_scalar(slot_e[:, :], slot_n[:, :], float(E - 1), None, ALU.min))
            do(v.tensor_scalar(slot_ne[:, :], slot_e[:, :], -1.0, float(E), ALU.mult, ALU.add))
            dc.end()
            v.tensor_copy(slot_ei[:, :], slot_e[:, :])
            v.scalar_tensor_tensor(out=slot_row[:, :], in0=slotno[:, :], scalar=float(P), in1=slot_r[:, :],
                                   op0=ALU.mult, op1=ALU.add).then_inc(table_ready, 1)

            def tile(k, par, half):
                if within(k, SLOTS):
                    dve.wait_ge(xsTh_ready, k + 1)
                    v.tensor_tensor(xsTl[:, par, :], ps_xsT[:, 0:P], xsTh[:, par, :].bitcast(F32), ALU.subtract)\
                     .then_inc(xsT_ready, 1)
                if within(k - 1, SLOTS):
                    dve.wait_ge(silu_ready, k)
                    dve.wait_ge(u_psum, k)
                    wait(dve, hT_psum, k - 2)
                    v.tensor_tensor(h[:, 1 - par, :], ps_u[:, :], sg, ALU.mult).then_inc(h_ready, 1)
                if within(k - 2, SLOTS):
                    if not isinstance(k, int):
                        dve.wait_ge(ys_out[par], 8 * (k - 2 - par))
                    elif k - 2 >= 2:
                        dve.wait_ge(ys_out[par], 16 * ((k - 2) // 2))
                    dve.wait_ge(row_known, k - 1)
                    v.tensor_copy(yrow[:, par:par + 1], row[:, par:par + 1]).then_inc(yrow_ready, 1)
                if within(k, SLOTS):
                    dve.wait_ge(xs_in[par], 16 * half + 16)
                    wait(dve, yrow_ready, k - 1)
                    ne = slot_ne[:, k:k + 1] if isinstance(k, int) else slot_ne[:, bass.ds(k, 1)]
                    v.scalar_tensor_tensor(out=row[:, par:par + 1], in0=xs[:, par, D + 1:D + 2], scalar=ne,
                                           in1=xs[:, par, D:D + 1], op0=ALU.not_equal, op1=ALU.add).then_inc(row_known, 1)

            pipeline(dve, SLOTS, 3, tile)

            dve.wait_ge(ys_ready, SLOTS)

            def combine(t, par, half):
                m, b, r = t - 1, t - 2, t - 3
                acc_own = Own(dve, own["acc"], 3 * J + 1, b)
                has_b = within(b, NB)
                if has_b:
                    gate = [gates_all[:, b * 8 + n:b * 8 + n + 1] if isinstance(b, int)
                            else gates_all[:, bass.ds(b * 8 + n, 1)] for n in range(SEL * J)]

                def hidden(c):
                    if within(m, NB):
                        dve.wait_ge(fsilu, C * m + (c + 1))
                        wait(dve, down_done, C * m + (c - 1))
                        v.tensor_tensor(fh[:, c % 2, :], ps_fu[c % 2][:, :], fsg[:, c % 2, :], ALU.mult)\
                         .then_inc(fh_ready, 1)

                hidden(0)
                if has_b:
                    dve.wait_ge(down_done, C * (b + 1))
                    dve.wait_ge(y2_in[par], 8 * (b - par) + 16 if not isinstance(b, int) else 16 * (b // 2) + 16)
                    for j in range(J):
                        acc_own.did(v.scalar_tensor_tensor(out=acc[:, j, :], in0=y2[:, par, j, 0:D], scalar=gate[j],
                                                           in1=ps_sh[par][:, j * P:(j + 1) * P], op0=ALU.mult, op1=ALU.add))
                hidden(1)
                if has_b:
                    acc_own.settle()
                    wait(dve, fn_ready, b - 1)
                    for j in range(J):
                        acc_own.did(v.scalar_tensor_tensor(out=acc2[:, par, j, :], in0=y2[:, par, j, D:2 * D],
                                                           scalar=gate[J + j], in1=acc[:, j, :], op0=ALU.mult, op1=ALU.add))
                hidden(2)
                if has_b:
                    acc_own.settle()
                    dve.sem_inc(dve_passed, 1)
                    for j in range(J):
                        acc_own.did(v.bn_stats(st2[:, j, :], acc2[:, par, j, :]))
                if within(t, NB):
                    dve.wait_ge(fxTh_ready, t + 1)
                    v.tensor_tensor(fxTl[:, par, :], fxT[:, par, :], fxTh[:, par, :].bitcast(F32), ALU.subtract)\
                     .then_inc(fxT_ready, 1)
                hidden(3)
                if within(r, NB):
                    dve.wait_ge(fn_ready, r + 1)
                    wait_turns(dve, out_done, 16, r, 1 - par)
                    v.tensor_tensor(res[:, 1 - par, :].rearrange("p (j d) -> p j d", d=D), fn, xcols(r), ALU.add)\
                     .then_inc(res_ready, 1)
                if has_b:
                    acc_own.settle()
                    dve.sem_inc(dve_passed, 1)
                    for j in range(J):
                        last = v.bn_aggr(mv2[:, j, :], st2[:, j, :])
                    acc_own.did(last)
                    acc_own.settle()
                    acc_own.end()
                    wait(dve, fn_ready, b)
                    v.tensor_scalar(veps2[:, :], mv2[:, :, 1], EPS, None, ALU.add).then_inc(shared_used, 1)
                    v.tensor_scalar(nmean2[:, :], mv2[:, :, 0], -1.0, None, ALU.mult).then_inc(fstats, 1)

            pipeline(dve, NB, 3, combine)


_INS = ['L0_attn_x', 'L0_attn_Wr', 'L0_attn_Wk', 'L0_attn_Wv', 'L0_attn_Wo', 'L0_attn_r_mu', 'L0_attn_k_mu',
        'L0_attn_v_mu', 'L0_attn_w', 'L0_attn_u', 'L0_ffn_gate_W', 'L0_ffn_w1_e', 'L0_ffn_w3_e', 'L0_ffn_w2_e',
        'L0_ffn_w1_s', 'L0_ffn_w3_s', 'L0_ffn_w2_s']
_OUTS = [((16, 512, 128), 'float32')]


def kernel(**inputs):
    import numpy as _np
    import concourse.bacc as _bacc
    from concourse import mybir as _mybir
    from concourse.bass_utils import run_bass_kernel_spmd as _run

    nc = _bacc.Bacc("TRN2", target_bir_lowering=False, num_devices=1)
    arrays, args = {}, []
    for name in _INS:
        a = _np.ascontiguousarray(inputs[name])
        arrays[f"in_{name}_dram"] = a
        args.append(nc.dram_tensor(f"in_{name}_dram", a.shape, _mybir.dt.from_np(a.dtype), kind="ExternalInput").ap())
    for i, (shape, dtype) in enumerate(_OUTS):
        dt = _mybir.dt.from_np(_np.dtype(dtype))
        args.append(nc.dram_tensor(f"out_{i}_dram", shape, dt, kind="ExternalOutput").ap())
    build(nc, *args)
    r = _run(nc, [arrays], core_ids=[0])
    return r.results[0]["out_0_dram"]
```

```python
from contextlib import ExitStack

import concourse.bass as bass
from concourse import mybir

F32 = mybir.dt.float32
F32R = mybir.dt.float32r
BF16 = mybir.dt.bfloat16
I32 = mybir.dt.int32
ALU = mybir.AluOpType
ACT = mybir.ActivationFunctionType
AX_X = mybir.AxisListType.X

P = 128
EPS = 1e-5
LOWEST = -3.0e38
CONSTS = 21


def wait(eng, sem, value):
    if isinstance(value, int) and value <= 0:
        return
    eng.wait_ge(sem, value)


class Own:

    def __init__(self, eng, sem, per, step, passed=None):
        self.eng, self.sem, self.per, self.base, self.n, self.passed = eng, sem, per, step * per, 0, passed

    def did(self, ins):
        self.n += 1
        ins.then_inc(self.sem, 1)

    def settle(self):
        self.eng.wait_ge(self.sem, self.base + self.n)
        if self.passed is not None:
            self.eng.sem_inc(self.passed, 1)

    def end(self):
        assert self.n == self.per, (self.n, self.per)


def pipeline(eng, count, skew, step, turn=2, unroll=None, new_turn=lambda: None):
    unroll = unroll or turn
    first, last = skew + skew % 2 + 2, count - count % 2
    last -= (last - first) % unroll
    for t in range(first):
        step(t, t % turn, t // turn)
    with eng.Fori(0, (last - first) // unroll) as i:
        new_turn()
        for n in range(first, first + unroll):
            step(unroll * i + n, n % turn, unroll // turn * i + n // turn)
    new_turn()
    for t in range(last, count + skew):
        step(t, t % turn, t // turn)


def within(t, count):
    return not isinstance(t, int) or 0 <= t < count


def early(b, count):
    return isinstance(b, int) and b < count


def wait_turns(eng, sems, amount, n, at):
    if isinstance(n, int):
        wait(eng, sems[at], amount * (n // len(sems)))
    else:
        eng.wait_ge(sems[at], amount // len(sems) * (n - at))


def build(nc, x_d, Wr_d, Wk_d, Wv_d, Wo_d, rmu_d, kmu_d, vmu_d, w_d, u_d,
          gate_d, w1_d, w3_d, w2_d, w1s_d, w3s_d, w2s_d, out_d):
    NB, T, D = x_d.shape
    E, _, F = w1_d.shape
    NS, _, FS = w1s_d.shape
    J = T // P
    C = F // P
    SEL = 2
    TOK = NB * T
    EARLY, EARLY_SPLIT = 1, 2
    MIX_END = NB + 4
    GROUPS = [(0, 1), (1, 4)] + [(b, b + 4) for b in range(4, NB, 4)]
    SPLITS = 2 * E + 2
    assert D == P and NS * FS == F and NB % 2 == 0 and T == F == 512
    REGION = TOK + P
    SLOTS = (SEL * TOK - E) // P + E
    ROWS = E * REGION + E * P
    XW = D + 2
    NOWHERE = float(4 * TOK)

    x_t = x_d.rearrange("b (j p) d -> b p j d", p=P)
    out_t = out_d.rearrange("b (j p) d -> b p j d", p=P)

    xs_d = nc.dram_tensor("xs_rows", [ROWS, XW], F32, kind="Internal").ap()
    ys_d = nc.dram_tensor("ys_rows", [SEL * TOK, D], F32, kind="Internal").ap()
    ys_t = ys_d.rearrange("(b j p k) d -> b p j (k d)", p=P, j=J, k=SEL)
    xfT_d = nc.dram_tensor("xfT_batches", [NB * P, T], F32, kind="Internal").ap()

    with ExitStack() as ctx:
        def sb(name, shape, dt=F32):
            return ctx.enter_context(nc.sbuf_tensor(name, shape, dt))

        def sem(name):
            return ctx.enter_context(nc.semaphore(name))

        def sem2(name):
            return [sem(name + "_even"), sem(name + "_odd")]

        bank = [ctx.enter_context(nc.psum_tensor(f"bank{n}", [P, 512], F32)) for n in range(8)]

        w13h = sb("w13h", [P, E, 2, F], F32R)
        w13l = sb("w13l", [P, E, 2, F], F32R)
        w2 = sb("w2", [P, E, C, D])
        stage = w2[:, :, :, :].rearrange("p (a e) c d -> p a e (c d)", a=2)
        sh_h = sb("sh_h", [P, 2, F], F32R)
        sh_l = sb("sh_l", [P, 2, F], F32R)
        w2s = sb("w2s", [P, C, D])
        raw = sb("raw", [P, 4, P])
        gate_raw = sb("gate_raw", [E, P])
        mix_w = sb("mix_w", [P, 3, 2, P])
        woT = sb("woT", [P, P])
        gateT = sb("gateT", [P, E])
        mu = sb("mu", [P, 3])
        omu = sb("omu", [P, 3])
        wvec = sb("wvec", [P, 1])
        uvec = sb("uvec", [P, 1])
        eu = sb("eu", [P, 1])
        decay = sb("decay", [P, T])
        grow = sb("grow", [P, T])
        ident = sb("ident", [P, P])
        upper = sb("upper", [P, P], BF16)
        ones = sb("ones", [P, P], BF16)
        zrow = sb("zrow", [P, XW])
        first = sb("first", [P, J, E])
        cnt = sb("cnt", [P, T])
        mhalf = sb("mhalf", [P, 4 * J])

        x_all = sb("x_all", [P, NB, J * D])
        gates_all = sb("gates_all", [P, NB * 8])

        xn = sb("xn", [P, J, D])
        xT = sb("xT", [P, 2, T + 2])
        ek = sb("ek", [P, 2, T])
        enk = sb("enk", [P, 2, T])
        th = sb("th", [P, 2, T])
        ekv = sb("ekv", [P, T])
        Aprev = sb("Aprev", [P, T])
        Bprev = sb("Bprev", [P, T])
        ekcnt = sb("ekcnt", [P, 2, T])
        vb = sb("vb", [P, T])
        wfull = vb
        y = sb("y", [P, 2, T])
        an = sb("an", [P, J, D])
        xf = sb("xf", [P, 2, J, XW])
        xfT = sb("xfT", [P, 2, T])
        st1 = sb("st1", [P, 4 * J, 6])
        mv1 = sb("mv1", [P, NB * J, 2])
        veps1, nmean1 = sb("veps1", [P, NB * J]), sb("nmean1", [P, NB * J])
        rstd1, nbias1 = sb("rstd1", [P, NB * J]), sb("nbias1", [P, NB * J])
        st3 = sb("st3", [P, J, 6])
        mv3 = sb("mv3", [P, 2, J, 2])
        veps3, nmean3 = sb("veps3", [P, 2, J]), sb("nmean3", [P, 2, J])
        rstd3, nbias3 = sb("rstd3", [P, 2, J]), sb("nbias3", [P, 2, J])
        st2 = sb("st2", [P, J, 6])
        mv2 = sb("mv2", [P, J, 2])
        veps2, nmean2 = sb("veps2", [P, J]), sb("nmean2", [P, J])
        rstd2, nbias2 = sb("rstd2", [P, J]), sb("nbias2", [P, J])

        lmax = sb("lmax", [P, J])
        ldiff = sb("ldiff", [P, J, E])
        expl = sb("expl", [P, 2, J * E])
        cand = sb("cand", [P, J, E])
        rest = sb("rest", [P, J, E])
        rmax = sb("rmax", [P, J])
        cand2 = sb("cand2", [P, J, E])
        cand3 = sb("cand3", [P, J, E])
        cbest2 = sb("cbest2", [P, J])
        chosen = sb("chosen", [P, SEL, J * E])
        both = sb("both", [P, J * E], BF16)
        nextrow = sb("nextrow", [P, E])
        rank = sb("rank", [P, J, E])
        picked = sb("picked", [P, SEL * J, E])
        posf = sb("posf", [P, SEL * J])
        idx = sb("idx", [P, 2, SEL * J], I32)
        pickedg = sb("pickedg", [P, SEL * J, E])
        gsum = sb("gsum", [P, SEL, J])
        zsum = sb("zsum", [P, J])
        zinv = sb("zinv", [P, J])

        nextrow_i = sb("nextrow_i", [P, E], I32)
        region0 = sb("region0", [P, E])
        tcount = sb("tcount", [P, E])
        tnum = sb("tnum", [P, E])
        tend = sb("tend", [P, E])
        tjump = sb("tjump", [P, E])
        one8 = sb("one8", [P, E])
        slotno = sb("slotno", [P, SLOTS])
        edge0 = sb("edge0", [P, TOK // P])
        past = sb("past", [P, E, SLOTS])
        tedge = past[:, :, 0:TOK // P]
        slot_n = sb("slot_n", [P, SLOTS])
        slot_r = sb("slot_r", [P, SLOTS])
        slot_e = sb("slot_e", [P, SLOTS])
        slot_ne = sb("slot_ne", [P, SLOTS])
        slot_ei = sb("slot_ei", [P, SLOTS], I32)
        slot_row = sb("slot_row", [P, SLOTS], I32)

        xs = sb("xs", [P, 4, XW])
        xsTh = sb("xsTh", [P, 2, P], F32R)
        xsTl = sb("xsTl", [P, 2, P], F32R)
        sg = xT[:, 0, 0:F]
        h = ek
        hT = th
        ys = sb("ys", [P, 2, D])
        yrow = sb("yrow", [P, 4], I32)

        fxT = xfT
        fxTh = sb("fxTh", [P, 2, T], F32R)
        fxTl = sb("fxTl", [P, 2, T], F32R)
        fsg = ek
        fh = enk
        y2 = w2[:, 0:4, :, :].rearrange("p (q n) c d -> p q (n c d)", q=2).rearrange("p q (j n) -> p q j n", j=J)
        acc, acc2, fn = xn, ekcnt[:, :, :].rearrange("p q (j d) -> p q j d", d=D), xT[:, 0, 0:J * D].rearrange("p (j d) -> p j d", d=D)
        res = y

        consts, consts0 = sem("consts"), sem("consts0")
        w_small, w_big = sem("w_small"), sem("w_big")
        turned, setup_act, setup_dve = sem("turned"), sem("setup_act"), sem("setup_dve")
        x_in, w13_in = [sem(f"x_in{n}") for n in range(len(GROUPS))], [sem(f"w13_in{n}") for n in range(5)]
        xfT_out, scattered, residual_done = sem2("xfT_out"), sem2("scattered"), sem("residual_done")
        hi_ready, lo_ready = sem("hi_ready"), sem("lo_ready")
        ln1_stats, ln1_rstd = sem("ln1_stats"), sem("ln1_rstd")
        ln3_stats, ln3_rstd = sem("ln3_stats"), sem("ln3_rstd")
        ln2_stats, ln2_rstd = sem("ln2_stats"), sem("ln2_rstd")
        xn_ready, xT_psum, xT_ready = sem("xn_ready"), sem("xT_psum"), sem("xT_ready")
        rk_psum, v_psum, exps_ready = sem("rk_psum"), sem("v_psum"), sem("exps_ready")
        ekcnt_ready, y_ready, attn_psum, an_ready = sem("ekcnt_ready"), sem("y_ready"), sem("attn_psum"), sem("an_ready")
        xf_ready, xfT_psum, xfT_ready = sem("xf_ready"), sem("xfT_psum"), sem("xfT_ready")
        logits_psum, ldiff_ready, expl_ready = sem("logits_psum"), sem("ldiff_ready"), sem("expl_ready")
        both_ready, rank_psum, idx_ready = sem("both_ready"), sem("rank_psum"), sem("idx_ready")
        pads_ready, table_ready = sem("pads_ready"), sem("table_ready")
        padded, padded_unused = sem("padded"), sem("padded_unused")
        xs_in, ys_out = [sem(f"xs_in{n}") for n in range(4)], sem2("ys_out")
        xsT_psum, xsTh_ready, xsT_ready = sem("xsT_psum"), sem("xsTh_ready"), sem("xsT_ready")
        g_psum, u_psum, silu_ready, h_ready = sem("g_psum"), sem("u_psum"), sem("silu_ready"), sem("h_ready")
        hT_psum, hT_ready, y_psum, ys_ready = sem("hT_psum"), sem("hT_ready"), sem("y_psum"), sem("ys_ready")
        yrow_ready, w2s_ready = sem("yrow_ready"), sem("w2s_ready")
        f_in, y2_in, out_done = sem2("f_in"), sem2("y2_in"), sem2("out_done")
        fxTh_ready, fxT_ready = sem("fxTh_ready"), sem("fxT_ready")
        fgu_psum, fsilu, fh_ready = sem("fgu_psum"), sem("fsilu"), sem("fh_ready")
        down_done, shared_used = sem("down_done"), sem("shared_used")
        fstats, frstd, fn_ready, res_ready = sem("fstats"), sem("frstd"), sem("fn_ready"), sem("res_ready")
        own = {k: sem("own_" + k) for k in ("stats1", "ln3", "mix", "ln2", "route", "place", "table", "pool1", "pool3", "pool2",
                                            "acc", "poolf")}
        act_passed, pool_passed, dve_passed = sem("act_passed"), sem("pool_passed"), sem("dve_passed")

        block = ctx.enter_context(nc.Block())

        ps_xT, ps_xfT, ps_r, ps_k, ps_attn, ps_small = (bank[n] for n in (0, 1, 2, 3, 6, 7))
        ps_v = (bank[4], bank[5])
        ps_logits = ps_small[:, 0:J * E]
        ps_rank = ps_small[:, J * E:2 * J * E]
        ps_total = ps_small[:, 2 * J * E:2 * J * E + E]
        ps_xsT, ps_g, ps_u, ps_hT, ps_y = (bank[n] for n in (0, 1, 2, 3, 4))
        ps_fg, ps_fu, ps_sh = bank[0:2], bank[2:4], bank[5:7]

        def xcols(b):
            v = x_all[:, b, :] if isinstance(b, int) else x_all[:, bass.ds(b, 1), :].rearrange("p a n -> p (a n)")
            return v.rearrange("p (j d) -> p j d", d=D)

        def weight(n):
            half = E // 2
            raw_w = stage[:, n // half % 2, n % half, :]
            if n >= 2 * E:
                return sh_h[:, n - 2 * E, :], sh_l[:, n - 2 * E, :], raw_w
            return w13h[:, n % E, n // E, :], w13l[:, n % E, n // E, :], raw_w

        def first_groups(t):
            return {0: [1], 1: [2], 2: [3], 4: [4]}.get(t, []) if isinstance(t, int) else []

        def splits(t):
            if not isinstance(t, int):
                return ()
            half = E // 2
            return {1: range(0, E), 2: range(E, E + half), 3: range(E + half, 2 * E), 4: range(2 * E, SPLITS)}.get(t, ())

        def group_of(b):
            return sum(b >= end for _, end in GROUPS)

        @block.sync
        def _(sp):
            for n, wd in enumerate((Wr_d, Wk_d, Wv_d, Wo_d)):
                sp.dma_start(raw[:, n, :], wd).then_inc(w_small, 16)
            sp.dma_start(xcols(0), x_t[0]).then_inc(x_in[0], 16)
            sp.dma_start(gate_raw[:, :], gate_d).then_inc(w_small, 16)
            for n, vd in enumerate((rmu_d, kmu_d, vmu_d)):
                sp.dma_start(mu[:, n:n + 1], vd.rearrange("(d a) -> d a", a=1)).then_inc(w_small, 16)
            sp.dma_start(wvec[:, :], w_d.rearrange("(d a) -> d a", a=1)).then_inc(w_small, 16)
            sp.dma_start(uvec[:, :], u_d.rearrange("(d a) -> d a", a=1)).then_inc(w_small, 16)

            def load_x(g):
                for b in range(*GROUPS[g]):
                    sp.dma_start(xcols(b), x_t[b]).then_inc(x_in[g], 16)

            def load_w13(n):
                wait(sp, lo_ready, E // 2 * (n - 1))
                if n == 4:
                    for k, wd in enumerate((w1s_d, w3s_d)):
                        sp.dma_start(stage[:, n % 2, k, :].rearrange("p (n f) -> p n f", f=FS), wd.rearrange("n d f -> d n f"))\
                          .then_inc(w13_in[n], 16)
                else:
                    some = slice(n % 2 * (E // 2), (n % 2 + 1) * (E // 2))
                    sp.dma_start(stage[:, n % 2, :, :], (w3_d if n // 2 else w1_d)[some].rearrange("e d f -> d e f"))\
                      .then_inc(w13_in[n], 16)

            for load, n in ((load_x, 1), (load_w13, 0), (load_w13, 1), (load_x, 2), (load_x, 3),
                            (load_w13, 2), (load_x, 4), (load_w13, 3), (load_w13, 4)):
                load(n)
            sp.wait_ge(lo_ready, SPLITS)
            sp.dma_start(w2[:, :, :, :], w2_d.rearrange("e (c f) d -> f e c d", f=P)).then_inc(w_big, 16)
            sp.dma_start(w2s[:, :, :], w2s_d.rearrange("n f d -> (n f) d").rearrange("(c f) d -> f c d", f=P))\
              .then_inc(w_big, 16)

            def load_f(n, par):
                sp.dma_start(fxT[:, par, :], xfT_d[n * P:(n + 1) * P, :] if isinstance(n, int)
                             else xfT_d[bass.ds(n * P, P), :]).then_inc(f_in[par], 16)

            def load_early(n):
                sp.wait_ge(xfT_out[n], NB // 2 * 16)
                sp.wait_ge(logits_psum, NB - 1 + n)
                load_f(n, n)

            def mix(t, par, half):
                if isinstance(t, int) and t == MIX_END:
                    load_early(0)
                c = t - 5
                if within(c, NB):
                    sp.wait_ge(xfT_ready, c + 1)
                    sp.dma_start(xfT_d[c * P:(c + 1) * P, :] if isinstance(c, int) else xfT_d[bass.ds(c * P, P), :],
                                 xfT[:, 1 - par, :]).then_inc(xfT_out[1 - par], 16)
            pipeline(sp, NB, 5, mix)
            for n in range(1, EARLY_SPLIT):
                load_early(n)

            sp.wait_ge(pads_ready, 1)
            for e in range(E):
                row = sp.value_load(nextrow_i[0:1, e:e + 1], min_val=0, max_val=E * REGION - P)
                sp.dma_start(xs_d[bass.ds(row, P), :], zrow[:, :]).then_inc(padded, 16)

            sp.wait_ge(table_ready, 1)
            for q in range(2):
                sp.wait_ge(scattered[q], NB // 2 * SEL * J * 16)
            sp.wait_ge(padded, E * 16)
            sp.wait_ge(padded_unused, 16)

            def load_slot(k, at, turn):
                if within(k, SLOTS):
                    wait(sp, xsT_psum, k - 3)
                    wait(sp, yrow_ready, k - 3)
                    row = sp.value_load(slot_row[0:1, k:k + 1] if isinstance(k, int) else slot_row[0:1, bass.ds(k, 1)],
                                        min_val=0, max_val=ROWS - P)
                    sp.dma_start(xs[:, at, :], xs_d[bass.ds(row, P), :]).then_inc(xs_in[at], 16)

            pipeline(sp, SLOTS, 4, load_slot, turn=4)

            def carry(n, par, half):
                if isinstance(n, int) and n == 1:
                    for q in range(2):
                        sp.wait_ge(ys_out[q], (SLOTS + 1 - q) // 2 * 16)
                b = n - 1
                if within(b, NB):
                    wait(sp, shared_used, b - 1)
                    src = ys_t[b] if isinstance(b, int) else ys_t[bass.ds(b, 1)].rearrange("a p j d -> p (a j) d")
                    sp.dma_start(y2[:, 1 - par, :, :], src).then_inc(y2_in[1 - par], 16)
                o = n - 4
                if within(o, NB):
                    sp.wait_ge(res_ready, o + 1)
                    dst = out_t[o] if isinstance(o, int) else out_t[bass.ds(o, 1)].rearrange("a p j d -> p (a j) d")
                    sp.dma_start(dst, res[:, par, :].rearrange("p (j d) -> p j d", d=D)).then_inc(out_done[par], 16)
                if within(n + 2, NB):
                    sp.wait_ge(fxT_ready, n + 1)
                    load_f(n + 2, par)

            pipeline(sp, NB - 2, 6, carry)
            for q in range(2):
                sp.wait_ge(out_done[q], NB // 2 * 16)

        @block.gpsimd
        def _(pool):
            g = nc.gpsimd
            g.memset(ident[:, :], 0.0).then_inc(consts0, 1)
            g.memset(upper[:, :], 0.0).then_inc(consts0, 1)
            n = 0

            def const(ins):
                nonlocal n
                n += 1
                ins.then_inc(consts, 1)

            def numbers(out, pattern, base=0, per_partition=0):
                const(g.iota(out, pattern=pattern, base=base, channel_multiplier=per_partition,
                             allow_small_or_imprecise_dtypes=True))

            for tile, value in ((ones[:, :], 1.0), (zrow[:, 0:D], 0.0), (zrow[:, D:D + 1], NOWHERE),
                                (zrow[:, D + 1:XW], 0.0), (mhalf[:, :], -0.5), (one8[:, :], 1.0),
                                (xT[:, 0, 0:2], 0.0), (xT[:, 1, 0:2], 0.0), (Aprev[:, 0:2], 0.0), (Bprev[:, 0:2], 0.0),
                                (cnt[:, 0:1], 0.0)):
                const(g.memset(tile, value))
            numbers(first[:, :, :], [[0, J], [-1, E]], base=E)
            numbers(cnt[:, 1:T], [[1, T - 1]])
            numbers(nextrow[:, :], [[REGION, E]])
            numbers(region0[:, :], [[REGION, E]])
            numbers(slotno[:, :], [[1, SLOTS]])
            numbers(edge0[:, :], [[P, TOK // P]])
            for q in range(2):
                numbers(xf[:, q, :, D], [[2 * P, J]], base=2 * T * (q - 2), per_partition=2)
            pool.wait_ge(consts0, 2)
            const(g.affine_select(out=ident[:, :], in_=ident[:, :], compare_op=ALU.not_equal, fill=1.0, base=0,
                                  pattern=[[-1, P]], channel_multiplier=1))
            const(g.affine_select(out=upper[:, :], in_=upper[:, :], compare_op=ALU.is_ge, fill=1.0, base=0,
                                  pattern=[[-1, P]], channel_multiplier=1))
            assert n == CONSTS
            pool.wait_ge(consts, CONSTS)
            pool.dma_start(xs_d[E * REGION:ROWS, :].rearrange("(a p) d -> p a d", p=P),
                           zrow[:, :].rearrange("p (a d) -> p a d", a=1).to_broadcast([P, E, XW])).then_inc(padded_unused, 16)

            def rsqrt(me, stats_sem, count, ve, nm, rs, nb, done, width):
                pool.wait_ge(stats_sem, count)
                pool.sem_inc(pool_passed, 1)
                me.did(g.tensor_tensor(rs, ve, mhalf[:, 0:width], ALU.pow))
                me.settle()
                g.tensor_tensor(nb, nm, rs, ALU.mult).then_inc(done, 1)
                me.end()

            def rsqrt1(g):
                tiles = slice(GROUPS[g][0] * J, GROUPS[g][1] * J)
                rsqrt(Own(pool, own["pool1"], 1, g, pool_passed), ln1_stats, g + 1,
                      veps1[:, tiles], nmean1[:, tiles], rstd1[:, tiles], nbias1[:, tiles], ln1_rstd,
                      tiles.stop - tiles.start)

            rsqrt1(0)

            def step(t, par, half):
                m, b, r, c, d = t - 2, t - 3, t - 4, t - 5, t - 6

                def scatter(k, q):
                    for j in range(J):
                        pool.indirect_dma_start(
                            xs_d[:, :], bass.IndirectOffsetOnAxis(ap=idx[:, q, k * J + j:k * J + j + 1], axis=0),
                            xf[:, q, j, :], None).then_inc(scattered[q], 16)

                if within(d, NB):
                    scatter(1, par)
                if within(r, NB):
                    rsqrt(Own(pool, own["pool3"], 1, r, pool_passed), ln3_stats, r + 1,
                          veps3[:, par, :], nmean3[:, par, :], rstd3[:, par, :], nbias3[:, par, :], ln3_rstd, J)
                if within(b, NB):
                    rsqrt(Own(pool, own["pool2"], 1, b, pool_passed), ln2_stats, b + 1,
                          veps2[:, :], nmean2[:, :], rstd2[:, :], nbias2[:, :], ln2_rstd, J)
                if within(m, NB):
                    pool.wait_ge(exps_ready, m + 1)
                    pool.sem_inc(pool_passed, 1)
                    wait(pool, y_ready, m - 1)
                    pool.sem_inc(pool_passed, 1)
                    g.tensor_tensor(ekcnt[:, par, :], ek[:, par, :], cnt[:, :], ALU.mult).then_inc(ekcnt_ready, 1)
                if within(c, NB):
                    pool.wait_ge(idx_ready, c + 1)
                    pool.sem_inc(pool_passed, 1)
                    scatter(0, 1 - par)
                for n in splits(t):
                    hi, lo, raw_w = weight(n)
                    pool.wait_ge(hi_ready, n + 1)
                    pool.sem_inc(pool_passed, 1)
                    g.tensor_tensor(lo, raw_w, hi.bitcast(F32), ALU.subtract).then_inc(lo_ready, 1)
                for group in first_groups(t):
                    rsqrt1(group)

            pipeline(pool, NB, 6, step)

            def spread(k, at, turn):
                pool.wait_ge(ys_ready, k + 1)
                pool.sem_inc(pool_passed, 1)
                pool.indirect_dma_start(ys_d[:, :], bass.IndirectOffsetOnAxis(ap=yrow[:, at:at + 1], axis=0),
                                        ys[:, at % 2, :], None, bounds_check=SEL * TOK - 1, oob_is_err=False)\
                    .then_inc(ys_out[at % 2], 16)

            pipeline(pool, SLOTS, 0, spread, turn=4)

            def last_norm(b, par, half):
                if within(b, NB):
                    rsqrt(Own(pool, own["poolf"], 1, b, pool_passed), fstats, b + 1,
                          veps2[:, :], nmean2[:, :], rstd2[:, :], nbias2[:, :], frstd, J)

            pipeline(pool, NB, 0, last_norm)

        @block.scalar
        def _(act):
            s = nc.scalar
            act.wait_ge(w_small, 160)
            s.activation(eu[:, :], uvec[:, :], ACT.Exp).then_inc(setup_act, 1)
            act.wait_ge(setup_dve, 2)
            s.activation(decay[:, :], wfull[:, :], ACT.Exp, scale=-1.0).then_inc(setup_act, 1)
            s.activation(grow[:, :], wfull[:, :], ACT.Exp).then_inc(setup_act, 1)
            act.wait_ge(consts, CONSTS)

            def tiles_of(small, b):
                return small[:, b * J:(b + 1) * J] if isinstance(b, int) else small[:, bass.ds(b * J, J)]

            def norm(dst, src, rs, nb):
                for j in range(J):
                    last = s.activation(dst(j), src[:, j, :], ACT.Identity, bias=nb[:, j:j + 1], scale=rs[:, j:j + 1])
                return last

            def split_f(t, par, half):
                act.wait_ge(f_in[par], 16 * half + 16)
                wait(act, fgu_psum, C * (t - 1))
                s.activation(fxTh[:, par, :], fxT[:, par, :], ACT.Copy).then_inc(fxTh_ready, 1)

            def silu(m, c):
                act.wait_ge(fgu_psum, C * m + (c + 1))
                wait(act, fh_ready, C * m + (c - 1))
                s.activation(fsg[:, c % 2, :], ps_fg[c % 2][:, :], ACT.Silu).then_inc(fsilu, 1)

            def step(t, par, half):
                a, m, b, r, c = t - 1, t - 2, t - 3, t - 4, t - 5
                q = 1 - par
                if isinstance(t, int) and t == MIX_END:
                    split_f(0, 0, 0)
                if within(c, NB):
                    wait(act, logits_psum, c - 1)
                    wait_turns(act, xfT_out, 16, c, q)
                    act.wait_ge(xfT_psum, c + 1)
                    s.activation(xfT[:, q, :], ps_xfT[:, :], ACT.Copy).then_inc(xfT_ready, 1)
                if within(m, NB):
                    act.wait_ge(rk_psum, m + 1)
                    wait(act, y_ready, m - 1)
                    wait(act, ekcnt_ready, m - 1)
                    s.activation(th[:, par, :], ps_r[:, :], ACT.Tanh, scale=0.5)
                    s.activation(enk[:, par, :], ps_k[:, :], ACT.Exp, scale=-1.0)
                    s.activation(ek[:, par, :], ps_k[:, :], ACT.Exp).then_inc(exps_ready, 1)
                if within(c, NB):
                    act.wait_ge(ldiff_ready, c + 1)
                    s.activation(expl[:, q, :], ldiff[:, :, :].rearrange("p j e -> p (j e)"), ACT.Exp)\
                     .then_inc(expl_ready, 1)
                if within(a, NB):
                    act.wait_ge(ln1_rstd, group_of(a) + 1 if isinstance(a, int) else len(GROUPS))
                    wait(act, xT_psum, a)
                    act.sem_inc(act_passed, 1)
                    norm(lambda j: xn[:, j, :], xcols(a), tiles_of(rstd1, a), tiles_of(nbias1, a)).then_inc(xn_ready, 1)
                    wait(act, v_psum, a - 1)
                    act.wait_ge(xT_psum, a + 1)
                    s.activation(xT[:, q, 2:T + 2], ps_xT[:, :], ACT.Copy).then_inc(xT_ready, 1)
                for n in splits(t):
                    if n % (E // 2) == 0:
                        act.wait_ge(w13_in[n // (E // 2)], 32 if n == 2 * E else 16)
                        act.sem_inc(act_passed, 1)
                    hi, _, raw_w = weight(n)
                    s.activation(hi, raw_w, ACT.Copy).then_inc(hi_ready, 1)
                if within(r, NB):
                    wait_turns(act, scattered, SEL * J * 16, r, par)
                    act.wait_ge(ln3_rstd, r + 1)
                    act.sem_inc(act_passed, 1)
                    norm(lambda j: xf[:, par, j, 0:D], xcols(r), rstd3[:, par, :], nbias3[:, par, :])\
                        .then_inc(xf_ready, 1)
                if within(b, NB):
                    wait(act, residual_done, b)
                    act.wait_ge(ln2_rstd, b + 1)
                    norm(lambda j: an[:, j, :], ps_attn[:, :].rearrange("p (j d) -> p j d", d=D), rstd2, nbias2)\
                        .then_inc(an_ready, 1)

            pipeline(act, NB, 5, step)

            act.wait_ge(y_ready, NB)
            act.wait_ge(v_psum, NB)

            for c in range(C):
                silu(0, c)
            for b in range(EARLY, EARLY_SPLIT):
                split_f(b, b, 0)

            def tile(k, par, half):
                if within(k - 4, SLOTS):
                    act.wait_ge(yrow_ready, k - 3)
                    wait_turns(act, ys_out, 16, k - 4, par)
                    act.wait_ge(y_psum, k - 3)
                    s.activation(ys[:, par, :], ps_y[:, 0:D], ACT.Copy).then_inc(ys_ready, 1)
                if within(k - 3, SLOTS):
                    wait(act, y_psum, k - 4)
                    act.wait_ge(hT_psum, k - 2)
                    s.activation(hT[:, 1 - par, :], ps_hT[:, :], ACT.Copy).then_inc(hT_ready, 1)
                if within(k - 1, SLOTS):
                    wait(act, h_ready, k - 1)
                    act.wait_ge(g_psum, k)
                    s.activation(sg, ps_g[:, :], ACT.Silu).then_inc(silu_ready, 1)
                if within(k, SLOTS):
                    wait(act, u_psum, k - 1)
                    act.wait_ge(xsT_psum, k + 1)
                    s.activation(xsTh[:, par, :], ps_xsT[:, 0:P], ACT.Copy).then_inc(xsTh_ready, 1)

            pipeline(act, SLOTS, 4, tile)

            act.wait_ge(h_ready, SLOTS)
            act.wait_ge(hT_psum, SLOTS)

            def shared(t, par, half):
                m, r = t - 1, t - 3

                has_m = within(m, NB) and not early(m, EARLY)

                def part(js):
                    if within(r, NB):
                        for j in js:
                            last = s.activation(fn[:, j, :], acc2[:, 1 - par, j, :], ACT.Identity,
                                                bias=nbias2[:, j:j + 1], scale=rstd2[:, j:j + 1])
                        return last

                if has_m:
                    silu(m, 0)
                if within(r, NB):
                    act.wait_ge(frstd, r + 1)
                    wait(act, res_ready, r)
                part(range(0, J // 2))
                if has_m:
                    silu(m, 1)
                last = part(range(J // 2, J))
                if within(r, NB):
                    last.then_inc(fn_ready, 1)
                if has_m:
                    silu(m, 2)
                if within(t, NB) and not early(t, EARLY_SPLIT):
                    split_f(t, par, half)
                if has_m:
                    silu(m, 3)

            pipeline(act, NB, 3, shared)

        @block.tensor
        def _(pe):
            p = nc.tensor
            pe.wait_ge(w_small, 160)
            pe.wait_ge(consts, CONSTS)
            for n in range(4):
                p.transpose(bank[0][:, n * P:(n + 1) * P], raw[:, n, :], ident[:, :])
            p.transpose(bank[1][:, 0:E], gate_raw[:, :], ident[0:E, 0:E]).then_inc(turned, 1)
            pe.wait_ge(setup_dve, 11)

            def split(dst, left, right):
                (lh, ll), (rh, rl) = left, right
                p.matmul(dst, ll, rh, start=True, stop=False)
                p.matmul(dst, lh, rl, start=False, stop=False)
                return p.matmul(dst, lh, rh, start=False, stop=True)

            def shared_up(b, q, c):
                wait(pe, fh_ready, C * b + (c - 1))
                x = (fxTh[:, q, :], fxTl[:, q, :])
                for n, dst in enumerate((ps_fg, ps_fu)):
                    last = split(dst[c % 2][:, :], (sh_h[:, n, c * P:(c + 1) * P], sh_l[:, n, c * P:(c + 1) * P]), x)
                last.then_inc(fgu_psum, 1)

            def shared_down(b, q, c):
                pe.wait_ge(fh_ready, C * b + (c + 1))
                if c == 0:
                    wait(pe, shared_used, b - 1)
                for j in range(J):
                    last = p.matmul(ps_sh[q][:, j * P:(j + 1) * P], fh[:, c % 2, j * P:(j + 1) * P], w2s[:, c, :],
                                    start=(c == 0 and j == 0), stop=(c == C - 1), skip_group_check=True)
                last.then_inc(down_done, 1)

            def step(t, par, half):
                a, m, b, c = t - 1, t - 2, t - 3, t - 5

                def project(n, dst):
                    p.matmul(dst[:, :], mix_w[:, n, 0, :], xT[:, par, 2:T + 2], start=True, stop=False)
                    return p.matmul(dst[:, :], mix_w[:, n, 1, :], xT[:, par, 1:T + 1], start=False, stop=True)

                if within(m, NB):
                    pe.wait_ge(xT_ready, m + 1)
                    wait(pe, exps_ready, m)
                    project(0, ps_r)
                if within(c, NB):
                    pe.wait_ge(xf_ready, c + 1)
                    wait(pe, xfT_ready, c)
                    for j in range(J):
                        last = p.transpose(ps_xfT[:, j * P:(j + 1) * P], xf[:, 1 - par, j, 0:D], ident[:, :])
                    last.then_inc(xfT_psum, 1)
                if within(m, NB):
                    project(1, ps_k).then_inc(rk_psum, 1)
                if within(c, NB):
                    pe.wait_ge(xfT_ready, c + 1)
                    wait(pe, idx_ready, c)
                    for j in range(J):
                        last = p.matmul(ps_logits[:, j * E:(j + 1) * E], xfT[:, 1 - par, j * P:(j + 1) * P], gateT[:, :],
                                        start=True, stop=True)
                    last.then_inc(logits_psum, 1)
                if within(b, NB):
                    pe.wait_ge(y_ready, b + 1)
                    wait(pe, an_ready, b)
                    for j in range(J):
                        last = p.matmul(ps_attn[:, j * P:(j + 1) * P], y[:, 1 - par, j * P:(j + 1) * P], woT[:, :],
                                        start=True, stop=True)
                    last.then_inc(attn_psum, 1)
                if isinstance(t, int) and t == MIX_END:
                    pe.wait_ge(lo_ready, 2 * E + 2)
                    pe.wait_ge(exps_ready, NB)
                    pe.wait_ge(fxT_ready, 1)
                    shared_up(0, 0, 0)
                if within(m, NB):
                    wait(pe, y_ready, m - 1)
                    project(2, ps_v[par]).then_inc(v_psum, 1)
                if within(a, NB):
                    pe.wait_ge(xn_ready, a + 1)
                    wait(pe, xT_ready, a)
                    for j in range(J):
                        last = p.transpose(ps_xT[:, j * P:(j + 1) * P], xn[:, j, :], ident[:, :])
                    last.then_inc(xT_psum, 1)
                if within(c, NB):
                    pe.wait_ge(both_ready, c + 1)
                    p.matmul(ps_rank, upper[:, :], both[:, :], start=True, stop=False)
                    for j in range(1, J):
                        p.matmul(ps_rank[:, j * E:J * E], ones[:, :], both[:, 0:(J - j) * E], start=False, stop=(j == J - 1))
                    for j in range(J):
                        last = p.matmul(ps_total, ones[:, :], both[:, j * E:(j + 1) * E], start=(j == 0), stop=(j == J - 1))
                    last.then_inc(rank_psum, 1)

            pipeline(pe, NB, 5, step)

            pe.wait_ge(an_ready, NB)
            pe.wait_ge(w2s_ready, 1)
            for c in range(1, C):
                shared_up(0, 0, c)
                shared_down(0, 0, c - 1)
            shared_down(0, 0, C - 1)

            pe.wait_ge(w_big, 32)
            pe.wait_ge(table_ready, 1)

            def expert(k):
                return pe.value_load(slot_ei[0:1, k:k + 1] if isinstance(k, int) else slot_ei[0:1, bass.ds(k, 1)],
                                     min_val=0, max_val=E - 1)

            known = []

            def tile(k, at, turn):
                q = 1 - at % 2

                def up(dst, n):
                    wh, wl = (w[:, bass.ds(known[-1], 1), n, :].rearrange("p a f -> p (a f)") for w in (w13h, w13l))
                    return split(dst[:, :], (xsTh[:, q, :], xsTl[:, q, :]), (wh, wl))

                known.append(expert(k - 1) if within(k - 1, SLOTS) else None)
                if within(k - 3, SLOTS):
                    wait(pe, h_ready, k - 2)
                    for c in range(C):
                        last = p.transpose(ps_hT[:, c * P:(c + 1) * P], h[:, q, c * P:(c + 1) * P], ident[:, :])
                    last.then_inc(hT_psum, 1)
                if within(k - 1, SLOTS):
                    if isinstance(k, int) and k == 1:
                        pe.wait_ge(xsT_ready, 1)
                    else:
                        pe.wait_ge(h_ready, k - 1)
                    up(ps_g, 0).then_inc(g_psum, 1)
                if within(k, SLOTS):
                    pe.wait_ge(xs_in[at], 16 * turn + 16)
                    p.transpose(ps_xsT[:, 0:P], xs[:, at, 0:D], ident[:, :]).then_inc(xsT_psum, 1)
                if within(k - 1, SLOTS):
                    up(ps_u, 1).then_inc(u_psum, 1)
                if within(k - 3, SLOTS):
                    e3 = known[-3] if len(known) >= 3 else expert(k - 3)
                    pe.wait_ge(hT_ready, k - 2)
                    for c in range(C):
                        last = p.matmul(ps_y[:, 0:D], hT[:, q, c * P:(c + 1) * P],
                                        w2[:, bass.ds(e3, 1), c, :].rearrange("p a d -> p (a d)"),
                                        start=(c == 0), stop=(c == C - 1))
                    last.then_inc(y_psum, 1)

            pipeline(pe, SLOTS, 3, tile, turn=4, unroll=8, new_turn=known.clear)

            pe.wait_ge(h_ready, SLOTS)

            def shared(m, par, half):
                has_m = within(m, NB) and not early(m, EARLY)
                if has_m:
                    pe.wait_ge(fxT_ready, m + 1)
                    shared_up(m, par, 0)
                if within(m - 1, NB) and not early(m - 1, EARLY):
                    shared_down(m - 1, 1 - par, C - 1)
                if has_m:
                    for c in range(1, C):
                        shared_up(m, par, c)
                        shared_down(m, par, c - 1)

            pipeline(pe, NB, 1, shared)

        @block.vector
        def _(dve):
            v = nc.vector
            stats1 = Own(dve, own["stats1"], NB * J + len(GROUPS), 0)

            def first_stats(g):
                start, stop = GROUPS[g]
                dve.wait_ge(x_in[g], 16 * (stop - start))
                dve.sem_inc(dve_passed, 1)
                for b in range(start, stop):
                    for j in range(J):
                        stats1.did(v.bn_stats(st1[:, (b - start) * J + j, :], xcols(b)[:, j, :]))
                stats1.settle()
                dve.sem_inc(dve_passed, 1)
                for n in range((stop - start) * J):
                    last = v.bn_aggr(mv1[:, start * J + n, :], st1[:, n, :])
                stats1.did(last)
                stats1.settle()
                tiles = slice(start * J, stop * J)
                v.tensor_scalar(veps1[:, tiles], mv1[:, tiles, 1], EPS, None, ALU.add)
                v.tensor_scalar(nmean1[:, tiles], mv1[:, tiles, 0], -1.0, None, ALU.mult).then_inc(ln1_stats, 1)

            first_stats(0)
            dve.wait_ge(w_small, 160)
            dve.wait_ge(consts, CONSTS)
            v.memset(wfull[:, :], 0.0).then_inc(setup_dve, 1)
            dve.wait_ge(setup_dve, 1)
            v.tensor_scalar(wfull[:, :], wfull[:, :], wvec[:, 0:1], None, ALU.add).then_inc(setup_dve, 1)
            v.tensor_scalar(omu[:, :], mu[:, :], -1.0, 1.0, ALU.mult, ALU.add).then_inc(setup_dve, 1)
            dve.wait_ge(setup_dve, 3)
            dve.wait_ge(turned, 1)
            for n in range(3):
                src = bank[0][:, n * P:(n + 1) * P]
                v.tensor_scalar(mix_w[:, n, 0, :], src, mu[:, n:n + 1], None, ALU.mult).then_inc(setup_dve, 1)
                v.tensor_scalar(mix_w[:, n, 1, :], src, omu[:, n:n + 1], None, ALU.mult).then_inc(setup_dve, 1)
            v.tensor_scalar(woT[:, :], bank[0][:, 3 * P:4 * P], 0.5, None, ALU.mult).then_inc(setup_dve, 1)
            v.tensor_copy(gateT[:, :], bank[1][:, 0:E]).then_inc(setup_dve, 1)
            dve.wait_ge(setup_act, 3)

            def over(small):
                return small.rearrange("p (j a) -> p j a", a=1).to_broadcast([P, J, E])

            def split_f(t, par):
                dve.wait_ge(fxTh_ready, t + 1)
                v.tensor_tensor(fxTl[:, par, :], fxT[:, par, :], fxTh[:, par, :].bitcast(F32), ALU.subtract)\
                 .then_inc(fxT_ready, 1)

            def hidden(m, c):
                dve.wait_ge(fsilu, C * m + (c + 1))
                wait(dve, down_done, C * m + (c - 1))
                v.tensor_tensor(fh[:, c % 2, :], ps_fu[c % 2][:, :], fsg[:, c % 2, :], ALU.mult).then_inc(fh_ready, 1)

            def step(t, par, half):
                m, b, r, c = t - 2, t - 3, t - 4, t - 5
                bp, rp, cp = 1 - par, par, 1 - par
                has_m, has_b, has_r, has_c = (within(n, NB) for n in (m, b, r, c))
                ln3 = Own(dve, own["ln3"], J + 1, r)
                mix = Own(dve, own["mix"], 6, b)
                mix.n = 2
                mix_next = Own(dve, own["mix"], 6, m)
                ln2 = Own(dve, own["ln2"], J + 1, b)
                rsd = Own(dve, residual_done, 1, r)
                route = Own(dve, own["route"], 10, c)
                place = Own(dve, own["place"], 10, c)
                one, two = (chosen[:, k, :].rearrange("p (j e) -> p j e", e=E) for k in range(SEL))
                logits = ps_logits.rearrange("p (j e) -> p j e", e=E)
                best = xf[:, cp, :, D + 1]

                def m_ekv():
                    dve.wait_ge(v_psum, m + 1)
                    mix_next.did(v.tensor_tensor(ekv[:, :], ps_v[par][:, :], ek[:, par, :], ALU.mult))

                def m_bprev():
                    dve.wait_ge(exps_ready, m + 1)
                    mix_next.did(v.tensor_tensor_scan(Bprev[:, 2:T], grow[:, 1:T - 1], enk[:, par, 1:T - 1], 0.0,
                                                      ALU.mult, ALU.add))

                def m_vb():
                    mix.settle()
                    mix.did(v.tensor_tensor(vb[:, :], ekv[:, :], Bprev[:, :], ALU.mult))

                def m_aprev():
                    mix.did(v.tensor_tensor_scan(Aprev[:, 2:T], decay[:, 1:T - 1], ekv[:, 1:T - 1], 0.0,
                                                 ALU.mult, ALU.add))

                def m_cnt():
                    mix.settle()
                    dve.wait_ge(ekcnt_ready, b + 1)
                    mix.did(v.tensor_tensor(vb[:, :], vb[:, :], ekcnt[:, bp, :], ALU.add))

                def m_wkv():
                    mix.settle()
                    mix.did(v.scalar_tensor_tensor(out=vb[:, :], in0=vb[:, :], scalar=eu[:, 0:1], in1=Aprev[:, :],
                                                   op0=ALU.mult, op1=ALU.add))

                def m_y():
                    mix.settle()
                    mix.end()
                    wait(dve, attn_psum, b - 1)
                    v.scalar_tensor_tensor(out=y[:, bp, :], in0=th[:, bp, :], scalar=1.0, in1=vb[:, :],
                                           op0=ALU.add, op1=ALU.mult).then_inc(y_ready, 1)

                def l_stats(j):
                    if j == 0:
                        dve.wait_ge(attn_psum, b + 1)
                        dve.sem_inc(dve_passed, 1)
                    ln2.did(v.bn_stats(st2[:, j, :], ps_attn[:, j * P:(j + 1) * P]))

                def l_aggr():
                    ln2.settle()
                    dve.sem_inc(dve_passed, 1)
                    for j in range(J):
                        last = v.bn_aggr(mv2[:, j, :], st2[:, j, :])
                    ln2.did(last)

                def l_done():
                    ln2.settle()
                    ln2.end()
                    wait(dve, an_ready, b)
                    v.tensor_scalar(veps2[:, :], mv2[:, :, 1], EPS, None, ALU.add)
                    v.tensor_scalar(nmean2[:, :], mv2[:, :, 0], -1.0, None, ALU.mult).then_inc(ln2_stats, 1)

                def r_max():
                    dve.wait_ge(logits_psum, c + 1)
                    route.did(v.tensor_reduce(lmax[:, :], logits, AX_X, ALU.max))

                def r_diff():
                    route.settle()
                    wait(dve, expl_ready, c)
                    v.tensor_tensor(ldiff[:, :, :], logits, over(lmax[:, :]), ALU.subtract).then_inc(ldiff_ready, 1)

                def r_cand():
                    dve.wait_ge(ldiff_ready, c + 1)
                    route.did(v.scalar_tensor_tensor(out=cand[:, :, :], in0=ldiff[:, :, :], scalar=0.0,
                                                     in1=first[:, :, :], op0=ALU.is_equal, op1=ALU.mult))

                def r_best():
                    route.settle()
                    wait_turns(dve, scattered, SEL * J * 16, c, cp)
                    route.did(v.tensor_reduce(best, cand[:, :, :], AX_X, ALU.max))

                def r_one():
                    route.settle()
                    route.did(v.tensor_tensor(one, cand[:, :, :], over(best), ALU.is_equal))

                def r_rest():
                    route.settle()
                    route.did(v.scalar_tensor_tensor(out=rest[:, :, :], in0=one, scalar=LOWEST, in1=ldiff[:, :, :],
                                                     op0=ALU.mult, op1=ALU.add))

                def r_rmax():
                    route.settle()
                    route.did(v.tensor_reduce(rmax[:, :], rest[:, :, :], AX_X, ALU.max))

                def r_cand2():
                    route.settle()
                    route.did(v.tensor_tensor(cand2[:, :, :], rest[:, :, :], over(rmax[:, :]), ALU.is_equal))

                def r_cand3():
                    route.settle()
                    route.did(v.tensor_tensor(cand3[:, :, :], cand2[:, :, :], first[:, :, :], ALU.mult))

                def r_best2():
                    route.settle()
                    route.did(v.tensor_reduce(cbest2[:, :], cand3[:, :, :], AX_X, ALU.max))

                def r_two():
                    route.settle()
                    route.did(v.tensor_tensor(two, cand3[:, :, :], over(cbest2[:, :]), ALU.is_equal))

                def r_both():
                    route.settle()
                    route.end()
                    v.tensor_tensor(both[:, :], chosen[:, 0, :], chosen[:, 1, :], ALU.add).then_inc(both_ready, 1)

                def twice(x):
                    return x.rearrange("p (a n) -> p a n", a=1).to_broadcast([P, SEL, J * E])

                def p_gates():
                    dve.wait_ge(expl_ready, c + 1)
                    place.did(v.tensor_tensor(pickedg[:, :, :].rearrange("p (k j) e -> p k (j e)", k=SEL), chosen[:, :, :],
                                              twice(expl[:, cp, :]), ALU.mult))
                    place.did(v.tensor_reduce(zsum[:, :], expl[:, cp, :].rearrange("p (j e) -> p j e", e=E), AX_X, ALU.add))
                    place.did(v.tensor_scalar(xf[:, cp, :, D], xf[:, cp, :, D], float(2 * 2 * T), None, ALU.add))

                def p_sums():
                    place.settle()
                    place.did(v.tensor_reduce(gsum[:, :, :].rearrange("p k j -> p (k j)"), pickedg[:, :, :], AX_X, ALU.add))
                    place.did(v.reciprocal(zinv[:, :], zsum[:, :]))

                def p_rank():
                    dve.wait_ge(rank_psum, c + 1)
                    place.did(v.tensor_tensor(rank[:, :, :], ps_rank.rearrange("p (j e) -> p j e", e=E),
                                              nextrow[:, :].rearrange("p (a e) -> p a e", a=1).to_broadcast([P, J, E]),
                                              ALU.add))

                def p_gates2():
                    place.settle()
                    place.did(v.tensor_tensor(nextrow[:, :], ps_total, nextrow[:, :], ALU.add))
                    eight = slice(c * 8, c * 8 + 8) if isinstance(c, int) else bass.ds(c * 8, 8)
                    place.did(v.scalar_tensor_tensor(
                        out=gates_all[:, eight].rearrange("p (k j) -> p k j", k=SEL), in0=gsum[:, :, :], scalar=0.5,
                        in1=zinv[:, :].rearrange("p (a j) -> p a j", a=1).to_broadcast([P, SEL, J]),
                        op0=ALU.mult, op1=ALU.mult))

                def p_pick():
                    place.did(v.tensor_tensor(picked[:, :, :].rearrange("p (k j) e -> p k (j e)", k=SEL), chosen[:, :, :],
                                              twice(rank[:, :, :].rearrange("p j e -> p (j e)")), ALU.mult))

                def p_rows():
                    place.settle()
                    place.did(v.tensor_reduce(posf[:, :], picked[:, :, :], AX_X, ALU.add))
                    place.settle()
                    place.end()
                    v.tensor_copy(idx[:, cp, :], posf[:, :]).then_inc(idx_ready, 1)

                def residual():
                    dve.wait_ge(an_ready, r + 1)
                    rsd.did(v.tensor_tensor(xcols(r), an[:, :, :], xcols(r), ALU.add))

                def third_stats(j):
                    if j == 0:
                        rsd.settle()
                        rsd.end()
                        dve.sem_inc(dve_passed, 1)
                    ln3.did(v.bn_stats(st3[:, j, :], xcols(r)[:, j, :]))

                def third_aggr():
                    ln3.settle()
                    dve.sem_inc(dve_passed, 1)
                    wait(dve, xf_ready, r - 1)
                    dve.sem_inc(dve_passed, 1)
                    for j in range(J):
                        last = v.bn_aggr(mv3[:, rp, j, :], st3[:, j, :])
                    ln3.did(last)
                    ln3.settle()
                    ln3.end()
                    v.tensor_scalar(veps3[:, rp, :], mv3[:, rp, :, 1], EPS, None, ALU.add)
                    v.tensor_scalar(nmean3[:, rp, :], mv3[:, rp, :, 0], -1.0, None, ALU.mult).then_inc(ln3_stats, 1)

                def run(has, *parts):
                    if has:
                        for part in parts:
                            part() if callable(part) else part[0](*part[1:])

                if isinstance(t, int) and t == MIX_END:
                    dve.wait_ge(w_big, 32)
                    v.tensor_scalar(w2s[:, :, :], w2s[:, :, :], 0.5 / NS, None, ALU.mult).then_inc(w2s_ready, 1)
                    split_f(0, 0)

                for has, *parts in (
                        (has_b, m_vb, m_aprev), (has_r, residual), (has_b, m_cnt), (has_r, (third_stats, 0)),
                        (has_b, m_wkv), (has_r, (third_stats, 1)), (has_b, m_y), (has_r, (third_stats, 2), (third_stats, 3)),
                        (has_r, third_aggr),
                        (has_b, (l_stats, 0)), (has_c, r_max), (has_b, (l_stats, 1)), (has_c, r_diff),
                        (has_b, (l_stats, 2)), (has_c, r_cand), (has_b, (l_stats, 3)), (has_c, r_best), (has_m, m_bprev),
                        (has_c, r_one), (has_b, l_aggr), (has_c, r_rest), (has_m, m_ekv), (has_c, r_rmax),
                        (has_b, l_done), (has_c, r_cand2, r_cand3, r_best2, r_two, r_both, p_gates, p_sums, p_rank,
                                          p_gates2, p_pick, p_rows)):
                    run(has, *parts)
                for g in first_groups(t):
                    first_stats(g)

            pipeline(dve, NB, 5, step)

            dc = Own(dve, own["table"], 11, 0)

            def do(ins):
                dc.did(ins)
                dc.settle()

            dve.wait_ge(own["place"], NB * 10)
            v.tensor_copy(nextrow_i[:, :], nextrow[:, :]).then_inc(pads_ready, 1)

            assert EARLY == 1 and C == 4
            hidden(0, 0)
            do(v.tensor_tensor(tcount[:, :], nextrow[:, :], region0[:, :], ALU.subtract))
            do(v.tensor_tensor(tedge[:, :, :],
                               tcount[:, :].rearrange("p (e a) -> p e a", a=1).to_broadcast([P, E, TOK // P]),
                               edge0[:, :].rearrange("p (a n) -> p a n", a=1).to_broadcast([P, E, TOK // P]), ALU.is_gt))
            do(v.tensor_reduce(tnum[:, :], tedge[:, :, :], AX_X, ALU.add))
            dc.did(v.tensor_tensor_scan(tend[:, :], one8[:, :], tnum[:, :], 0.0, ALU.mult, ALU.add))
            do(v.tensor_scalar(tjump[:, :], tnum[:, :], -float(P), float(REGION), ALU.mult, ALU.add))
            slots = slotno[:, :].rearrange("p (a n) -> p a n", a=1).to_broadcast([P, E, SLOTS])
            do(v.tensor_tensor(past[:, :, :], slots,
                               tend[:, :].rearrange("p (e a) -> p e a", a=1).to_broadcast([P, E, SLOTS]), ALU.is_ge))
            hidden(0, 1)
            dc.did(v.tensor_reduce(slot_n[:, :], past[:, :, :].rearrange("p e n -> p n e"), AX_X, ALU.add))
            dc.settle()
            do(v.tensor_tensor(past[:, :, :], past[:, :, :],
                               tjump[:, :].rearrange("p (e a) -> p e a", a=1).to_broadcast([P, E, SLOTS]), ALU.mult))
            hidden(0, 2)
            dc.did(v.tensor_reduce(slot_r[:, :], past[:, :, :].rearrange("p e n -> p n e"), AX_X, ALU.add))
            do(v.tensor_scalar(slot_e[:, :], slot_n[:, :], float(E - 1), None, ALU.min))
            do(v.tensor_scalar(slot_ne[:, :], slot_e[:, :], -1.0, float(E), ALU.mult, ALU.add))
            dc.end()
            v.tensor_copy(slot_ei[:, :], slot_e[:, :])
            v.scalar_tensor_tensor(out=slot_row[:, :], in0=slotno[:, :], scalar=float(P), in1=slot_r[:, :],
                                   op0=ALU.mult, op1=ALU.add).then_inc(table_ready, 1)
            hidden(0, 3)
            for b in range(EARLY, EARLY_SPLIT):
                split_f(b, b)

            def tile(k, at, turn):
                par = at % 2
                if within(k, SLOTS):
                    dve.wait_ge(xsTh_ready, k + 1)
                    v.tensor_tensor(xsTl[:, par, :], ps_xsT[:, 0:P], xsTh[:, par, :].bitcast(F32), ALU.subtract)\
                     .then_inc(xsT_ready, 1)
                if within(k - 1, SLOTS):
                    wait(dve, hT_psum, k - 2)
                    dve.wait_ge(silu_ready, k)
                    dve.wait_ge(u_psum, k)
                    v.tensor_tensor(h[:, 1 - par, :], ps_u[:, :], sg, ALU.mult).then_inc(h_ready, 1)
                if within(k, SLOTS):
                    dve.wait_ge(xs_in[at], 16 * turn + 16)
                    if not isinstance(k, int) or k >= 4:
                        wait_turns(dve, ys_out, 16, k - 2, par)
                    ne = slot_ne[:, k:k + 1] if isinstance(k, int) else slot_ne[:, bass.ds(k, 1)]
                    v.scalar_tensor_tensor(out=yrow[:, at:at + 1], in0=xs[:, at, D + 1:D + 2], scalar=ne,
                                           in1=xs[:, at, D:D + 1], op0=ALU.not_equal, op1=ALU.add).then_inc(yrow_ready, 1)

            pipeline(dve, SLOTS, 4, tile, turn=4)

            def combine(t, par, half):
                m, b, r = t - 1, t - 2, t - 3
                acc_own = Own(dve, own["acc"], 3 * J + 1, b)
                has_b = within(b, NB)
                if has_b:
                    gate = [gates_all[:, b * 8 + n:b * 8 + n + 1] if isinstance(b, int)
                            else gates_all[:, bass.ds(b * 8 + n, 1)] for n in range(SEL * J)]

                def shared(c):
                    if within(m, NB) and not early(m, EARLY):
                        hidden(m, c)

                def first_choice():
                    dve.wait_ge(down_done, C * (b + 1))
                    dve.wait_ge(y2_in[par], 8 * (b - par) + 16 if not isinstance(b, int) else 16 * (b // 2) + 16)
                    for j in range(J):
                        acc_own.did(v.scalar_tensor_tensor(out=acc[:, j, :], in0=y2[:, par, j, 0:D], scalar=gate[j],
                                                           in1=ps_sh[par][:, j * P:(j + 1) * P], op0=ALU.mult, op1=ALU.add))

                def second_choice():
                    acc_own.settle()
                    wait(dve, fn_ready, b - 1)
                    for j in range(J):
                        acc_own.did(v.scalar_tensor_tensor(out=acc2[:, par, j, :], in0=y2[:, par, j, D:2 * D],
                                                           scalar=gate[J + j], in1=acc[:, j, :], op0=ALU.mult, op1=ALU.add))

                def last_stats():
                    acc_own.settle()
                    dve.sem_inc(dve_passed, 1)
                    for j in range(J):
                        acc_own.did(v.bn_stats(st2[:, j, :], acc2[:, par, j, :]))

                woven = has_b and not early(b, EARLY)
                shared(0)
                if woven:
                    first_choice()
                shared(1)
                if woven:
                    second_choice()
                shared(2)
                if woven:
                    last_stats()
                if within(t, NB) and not early(t, EARLY_SPLIT):
                    split_f(t, par)
                shared(3)
                if within(r, NB):
                    dve.wait_ge(fn_ready, r + 1)
                    wait_turns(dve, out_done, 16, r, 1 - par)
                    v.tensor_tensor(res[:, 1 - par, :].rearrange("p (j d) -> p j d", d=D), fn, xcols(r), ALU.add)\
                     .then_inc(res_ready, 1)
                if has_b and not woven:
                    first_choice()
                    second_choice()
                    last_stats()
                if has_b:
                    acc_own.settle()
                    dve.sem_inc(dve_passed, 1)
                    for j in range(J):
                        last = v.bn_aggr(mv2[:, j, :], st2[:, j, :])
                    acc_own.did(last)
                    acc_own.settle()
                    acc_own.end()
                    wait(dve, fn_ready, b)
                    v.tensor_scalar(veps2[:, :], mv2[:, :, 1], EPS, None, ALU.add).then_inc(shared_used, 1)
                    v.tensor_scalar(nmean2[:, :], mv2[:, :, 0], -1.0, None, ALU.mult).then_inc(fstats, 1)

            pipeline(dve, NB, 3, combine)


_INS = ['L0_attn_x', 'L0_attn_Wr', 'L0_attn_Wk', 'L0_attn_Wv', 'L0_attn_Wo', 'L0_attn_r_mu', 'L0_attn_k_mu',
        'L0_attn_v_mu', 'L0_attn_w', 'L0_attn_u', 'L0_ffn_gate_W', 'L0_ffn_w1_e', 'L0_ffn_w3_e', 'L0_ffn_w2_e',
        'L0_ffn_w1_s', 'L0_ffn_w3_s', 'L0_ffn_w2_s']
_OUTS = [((16, 512, 128), 'float32')]


def kernel(**inputs):
    import numpy as _np
    import concourse.bacc as _bacc
    from concourse import mybir as _mybir
    from concourse.bass_utils import run_bass_kernel_spmd as _run

    nc = _bacc.Bacc("TRN2", target_bir_lowering=False, num_devices=1)
    arrays, args = {}, []
    for name in _INS:
        a = _np.ascontiguousarray(inputs[name])
        arrays[f"in_{name}_dram"] = a
        args.append(nc.dram_tensor(f"in_{name}_dram", a.shape, _mybir.dt.from_np(a.dtype), kind="ExternalInput").ap())
    for i, (shape, dtype) in enumerate(_OUTS):
        dt = _mybir.dt.from_np(_np.dtype(dtype))
        args.append(nc.dram_tensor(f"out_{i}_dram", shape, dt, kind="ExternalOutput").ap())
    build(nc, *args)
    r = _run(nc, [arrays], core_ids=[0])
    return r.results[0]["out_0_dram"]
```
